# Optimizing a Trainium2 kernel written in Bass

```python
import numpy as np
import jax
import jax.numpy as jnp

def _softmax(x, axis=-1):
    return jax.nn.softmax(x, axis=axis)

def _gelu(x):
    return jax.nn.gelu(x, approximate=True)

def _silu(x):
    return jax.nn.silu(x)

def _sigmoid(x):
    return jax.nn.sigmoid(x)

def _layernorm(x, axis=-1, eps=1e-05):
    m = jnp.mean(x, axis=axis, keepdims=True)
    v = jnp.var(x, axis=axis, keepdims=True)
    return (x - m) / jnp.sqrt(v + eps)

def _scatter_add(tgt, idx, src, axis=0):
    return tgt.at[idx].add(src)

def _segment_sum(src, seg, n):
    return jax.ops.segment_sum(src, seg, n)
kernel_name = 'mk_seq_postln_d1_jaxref_r8_d5901f'

def setup_inputs(seed: int=0):
    np.random.seed(seed)
    _w = jnp.asarray

    def _L0_attn_setup():
        import jax, jax.numpy as jnp
        import numpy as np
        import math
        B, T, C = (2, 256, 256)
        NH, L = (16, 128)
        key = jax.random.key(seed)
        ks = jax.random.split(key, 7)
        s = 0.02
        return {'x': jax.random.normal(ks[0], (B, T, C), dtype=jnp.float32), 'W_lat': jax.random.normal(ks[1], (C, L), dtype=jnp.float32) * s, 'b_lat': jnp.zeros((L,), dtype=jnp.float32), 'W_d': jax.random.normal(ks[2], (C, NH * L), dtype=jnp.float32) * s, 'b_d': jnp.zeros((NH * L,), dtype=jnp.float32), 'W_proj': jax.random.normal(ks[3], (NH * L, C), dtype=jnp.float32) * s, 'b_proj': jnp.zeros((C,), dtype=jnp.float32)}
    _L0_attn_in = _L0_attn_setup()

    def _L0_ffn_setup():
        import jax, jax.numpy as jnp
        import numpy as np
        B, S, D, DFF = (4, 512, 256, 1024)
        CAPACITY_FACTOR = 0.5
        K = int(CAPACITY_FACTOR * S)
        key = jax.random.key(seed)
        ks = jax.random.split(key, 5)
        hidden_states = jax.random.normal(ks[0], (B, S, D), dtype=jnp.float32)
        router_weight = jax.random.normal(ks[1], (D,), dtype=jnp.float32) * 0.02
        router_bias = jnp.zeros((1,), dtype=jnp.float32)
        w1 = jax.random.normal(ks[2], (D, DFF), dtype=jnp.float32) * (1.0 / np.sqrt(D))
        b1 = jnp.zeros((DFF,), dtype=jnp.float32)
        w2 = jax.random.normal(ks[3], (DFF, D), dtype=jnp.float32) * (1.0 / np.sqrt(DFF))
        b2 = jnp.zeros((D,), dtype=jnp.float32)
        return {'hidden_states': hidden_states, 'router_weight': router_weight, 'router_bias': router_bias, 'w1': w1, 'b1': b1, 'w2': w2, 'b2': b2}
    _L0_ffn_in = _L0_ffn_setup()
    _d = {'L0_attn_x': _L0_attn_in['x'], 'L0_attn_W_lat': _L0_attn_in['W_lat'], 'L0_attn_b_lat': _L0_attn_in['b_lat'], 'L0_attn_W_d': _L0_attn_in['W_d'], 'L0_attn_b_d': _L0_attn_in['b_d'], 'L0_attn_W_proj': _L0_attn_in['W_proj'], 'L0_attn_b_proj': _L0_attn_in['b_proj'], 'L0_ffn_router_weight': _L0_ffn_in['router_weight'], 'L0_ffn_router_bias': _L0_ffn_in['router_bias'], 'L0_ffn_w1': _L0_ffn_in['w1'], 'L0_ffn_b1': _L0_ffn_in['b1'], 'L0_ffn_w2': _L0_ffn_in['w2'], 'L0_ffn_b2': _L0_ffn_in['b2']}
    _x0 = _d['L0_attn_x']
    _d['L0_attn_x'] = jax.random.normal(jax.random.fold_in(jax.random.key(seed), 1), (2, 512, 256), dtype=_x0.dtype)
    del _x0
    return _d

def reference(L0_attn_x, L0_attn_W_lat, L0_attn_b_lat, L0_attn_W_d, L0_attn_b_d, L0_attn_W_proj, L0_attn_b_proj, L0_ffn_router_weight, L0_ffn_router_bias, L0_ffn_w1, L0_ffn_b1, L0_ffn_w2, L0_ffn_b2):

    def _L0_attn_ref(x, W_lat, b_lat, W_d, b_d, W_proj, b_proj):
        import jax, jax.numpy as jnp
        import numpy as np
        import math
        B, T, C = (2, 256, 256)
        NH, L = (16, 128)
        Bx, Tx, Cx = x.shape
        k = x @ W_lat + b_lat
        q = (x @ W_d + b_d).reshape(Bx, Tx, NH, L)
        q = jnp.transpose(q, (0, 2, 1, 3))
        scale = 1.0 / math.sqrt(L)
        att = jnp.einsum('bhtl,bsl->bhts', q, k) * scale
        causal = jnp.tril(jnp.ones((Tx, Tx), dtype=bool))
        att = jnp.where(causal[None, None], att, -jnp.inf)
        att = jax.nn.softmax(att, axis=-1)
        y = jnp.einsum('bhts,bsl->bhtl', att, k)
        y = jnp.transpose(y, (0, 2, 1, 3)).reshape(Bx, Tx, NH * L)
        return y @ W_proj + b_proj

    def _L0_ffn_ref(hidden_states, router_weight, router_bias, w1, b1, w2, b2):
        import jax, jax.numpy as jnp
        import numpy as np
        B, S, D, DFF = (4, 512, 256, 1024)
        CAPACITY_FACTOR = 0.5
        K = int(CAPACITY_FACTOR * S)
        b, s, d = hidden_states.shape
        scores = jnp.einsum('bsd,d->bs', hidden_states, router_weight) + router_bias[0]
        top_scores, indices = jax.lax.top_k(scores, K)
        weights = jax.nn.sigmoid(top_scores)
        selected = jnp.take_along_axis(hidden_states, indices[:, :, None], axis=1)
        h = jax.nn.gelu(jnp.einsum('bkd,df->bkf', selected, w1) + b1)
        processed = jnp.einsum('bkf,fd->bkd', h, w2) + b2
        weighted = processed * weights[:, :, None]
        flat = hidden_states.reshape(b * s, d)
        flat_idx = (indices + jnp.arange(b)[:, None] * s).reshape(-1)
        out = flat.at[flat_idx].add(weighted.reshape(b * K, d))
        return out.reshape(b, s, d)
    x = L0_attn_x
    x = _layernorm(x + _L0_attn_ref(x, L0_attn_W_lat, L0_attn_b_lat, L0_attn_W_d, L0_attn_b_d, L0_attn_W_proj, L0_attn_b_proj), axis=-1)
    x = _layernorm(x + _L0_ffn_ref(x, L0_ffn_router_weight, L0_ffn_router_bias, L0_ffn_w1, L0_ffn_b1, L0_ffn_w2, L0_ffn_b2), axis=-1)
    return x

_drawn_inputs = setup_inputs


def setup_inputs(seed=0):
    import zlib

    import numpy as np

    out = dict(_drawn_inputs(seed))
    spreads = {'L0_attn_b_lat': (0.0, 0.1),
     'L0_attn_b_d': (0.0, 2.0),
     'L0_attn_b_proj': (0.0, 0.1),
     'L0_ffn_b1': (0.0, 0.596),
     'L0_ffn_b2': (0.0, 0.411)}
    factors = {'L0_attn_W_d': 6.639}
    for name, (base, spread) in spreads.items():
        noise = np.random.default_rng([zlib.crc32(name.encode()), seed]).standard_normal(out[name].shape)
        drawn = base * np.exp(spread * noise) if base else spread * noise
        out[name] = jnp.asarray(drawn.astype(out[name].dtype))
    for name, factor in factors.items():
        out[name] = (out[name] * factor).astype(out[name].dtype)
    return out
```

```python
import math
from contextlib import ExitStack

import concourse.bass as bass
from concourse import mybir

F32 = mybir.dt.float32
F32R = mybir.dt.float32r
BF16 = mybir.dt.bfloat16
ACT = mybir.ActivationFunctionType
ALU = mybir.AluOpType
AX_X = mybir.AxisListType.X

P = 128
BATCH, SEQ, DIM = 2, 512, 256
HEADS, LAT = 16, 128
FFN = 1024
KEEP = SEQ // 2
TILES = SEQ // P
CH = DIM // P
FCH = FFN // P
RCH = KEEP // P
UNITS = BATCH * HEADS
SCALE = 1.0 / math.sqrt(LAT)
EPS = 1e-5
MASKED = -1.0e38
MIN_N = 256

P_OFF = [P * (j * (j + 1) // 2) for j in range(TILES)]
P_COLS = P * TILES * (TILES + 1) // 2
PT_OFF = {3: P, 2: 2 * P, 1: 4 * P, 0: 7 * P}
PT_COLS = 11 * P


def mk_layer_kernel(nc, x, W_lat, b_lat, W_d, b_d, W_proj, b_proj, router_w, router_b,
                    w1, b1, w2, b2, out):
    with ExitStack() as top:
        def sb(name, shape, dt=F32, stack=top):
            return stack.enter_context(nc.sbuf_tensor(name, shape, dt))

        def sem(name):
            return top.enter_context(nc.semaphore(name))

        x1 = sb("x1", [P, BATCH * TILES, DIM])
        W2_AT = CH * FFN
        wf_raw = sb("wf_raw", [P, W2_AT + FCH * DIM])
        wf_hi, wf_lo = (sb(n, [P, W2_AT + FCH * DIM], F32R) for n in ("wf_hi", "wf_lo"))
        WF_PART = (W2_AT + FCH * DIM) // UNITS
        ident = sb("ident", [P, P])
        ident_bf = sb("ident_bf", [P, P], BF16)
        mask_bf = sb("mask_bf", [P, P], BF16)
        earlier = sb("earlier", [P, (2 * TILES - 1) * P], BF16)
        iota_row = sb("iota_row", [P, KEEP])
        iota_col = sb("iota_col", [P, RCH])
        bias_rows = sb("bias_rows", [HEADS + 1 + FCH, P])
        bias_cols = sb("bias_cols", [P, HEADS + 1 + FCH])
        bproj_all = sb("bproj_all", [P, DIM])
        b2_all = sb("b2_all", [P, DIM])
        rw_all = sb("rw_all", [P, DIM])
        rb_all = sb("rb_all", [P, 1])
        minus_half = sb("minus_half", [P, TILES])
        negmax = sb("negmax", [P, 2, TILES])
        sums = sb("sums", [P, 2, TILES])
        rinv = sb("rinv", [P, 2, TILES])
        B_LAT = HEADS
        B_ONE = HEADS + 1

        bank = [top.enter_context(nc.psum_tensor(f"bank{i}", [P, 512], F32)) for i in range(6)]
        ps_s3, ps_s2, ps_s10, ps_t0, ps_t1, ps_qy = bank
        ps_out = top.enter_context(nc.psum_tensor("ps_out", [P, TILES, DIM], F32))

        x_in = [sem(f"x_in{b}") for b in range(BATCH)]
        wlat_in, bias_in, wp_in, w1_in, w2_in = (sem(n) for n in ("wlat_in", "bias_in", "wp_in", "w1_in", "w2_in"))
        wd_in = [sem("wd_in0"), sem("wd_in1")]
        rows_in = sem("rows_in")
        consts0, consts = sem("consts0"), sem("consts")
        prep_pe, prep_act, prep_dve, prep_pool = (sem(n) for n in ("prep_pe", "prep_act", "prep_dve", "prep_pool"))
        wd_hi_done, wd_split = sem("wd_hi_done"), sem("wd_split")
        wp_hi_done, wp_split = sem("wp_hi_done"), sem("wp_split")
        wf_hi_done, wf_split = sem("wf_hi_done"), sem("wf_split")
        q_ready, q_hi_done, q_lo_done = sem("q_ready"), sem("q_hi_done"), sem("q_lo_done")
        scores_ready, negmax_done, exp_done, rinv_done = (
            sem(n) for n in ("scores_ready", "negmax_done", "exp_done", "rinv_done"))
        norm_act, norm_dve, norm_pool = sem("norm_act"), sem("norm_dve"), sem("norm_pool")
        pt_ready, pt_hi_done, pt_lo_done = sem("pt_ready"), sem("pt_hi_done"), sem("pt_lo_done")
        y_ready, y_hi_done, y_lo_done = sem("y_ready"), sem("y_hi_done"), sem("y_lo_done")
        proj_done, out_taken = sem("proj_done"), sem("out_taken")
        stored = [sem(f"stored{b}") for b in range(BATCH)]

        def wait(eng, s, value):
            if not isinstance(value, int) or value > 0:
                eng.wait_ge(s, value)

        att = ExitStack()
        x_nat = sb("x_nat", [P, BATCH * TILES, DIM], F32, att)
        wlat_raw = sb("wlat_raw", [P, CH, LAT], F32, att)
        wlat_hi, wlat_lo = sb("wlat_hi", [P, CH, LAT], F32R, att), sb("wlat_lo", [P, CH, LAT], F32R, att)
        wd_raw = sb("wd_raw", [P, CH, HEADS * LAT], F32, att)
        wp_raw = sb("wp_raw", [P, HEADS * DIM], F32, att)
        xT_hi = [sb(f"xT_hi{b}", [P, CH, SEQ], F32R, att) for b in range(BATCH)]
        xT_lo = [sb(f"xT_lo{b}", [P, CH, SEQ], F32R, att) for b in range(BATCH)]
        kT = [sb(f"kT{b}", [P, SEQ], F32, att) for b in range(BATCH)]
        kT_hi = [sb(f"kT_hi{b}", [P, SEQ], F32R, att) for b in range(BATCH)]
        kT_lo = [sb(f"kT_lo{b}", [P, SEQ], F32R, att) for b in range(BATCH)]
        k_hi = [sb(f"k_hi{b}", [P, TILES, LAT], F32R, att) for b in range(BATCH)]
        k_lo = [sb(f"k_lo{b}", [P, TILES, LAT], F32R, att) for b in range(BATCH)]
        wd_hi = [sb(f"wd_hi{s}", [P, CH, LAT], F32R, att) for s in range(2)]
        wd_lo = [sb(f"wd_lo{s}", [P, CH, LAT], F32R, att) for s in range(2)]
        wp_hi = [sb(f"wp_hi{s}", [P, DIM], F32R, att) for s in range(2)]
        wp_lo = [sb(f"wp_lo{s}", [P, DIM], F32R, att) for s in range(2)]
        qT_hi, qT_lo = sb("qT_hi", [P, SEQ], F32R, att), sb("qT_lo", [P, SEQ], F32R, att)
        yT_hi, yT_lo = sb("yT_hi", [P, SEQ], F32R, att), sb("yT_lo", [P, SEQ], F32R, att)
        probs = [sb(f"probs{s}", [P, P_COLS], F32, att) for s in range(2)]
        pT_hi, pT_lo = sb("pT_hi", [P, PT_COLS], F32R, att), sb("pT_lo", [P, PT_COLS], F32R, att)

        def p_tile(s, j):
            return probs[s][:, P_OFF[j]:P_OFF[j] + (j + 1) * P]

        score_bank = {3: ps_s3[:, :], 2: ps_s2[:, 0:384], 1: ps_s10[:, MIN_N:2 * MIN_N], 0: ps_s10[:, 0:P]}

        turns = [([0], ps_t0, slice(PT_OFF[0], PT_OFF[0] + 4 * P)),
                 ([1], ps_t1, slice(PT_OFF[1], PT_OFF[1] + 3 * P)),
                 ([3, 2], ps_t0, slice(PT_OFF[3], PT_OFF[3] + 3 * P))]

        STAGES = (2, 1, 0, -1, -2)
        LOOP = 0

        def periods(eng, body):
            def at(p, fixed):
                body(p, fixed % 2, {k: (fixed + k) // HEADS for k in STAGES},
                     {k: 0 <= fixed + k < UNITS for k in STAGES})

            def loop(first):
                with eng.Fori(0, LOOP) as i:
                    for k in range(2):
                        at(i * 2 + (first + k), first + k)

            if not LOOP:
                for p in range(-1, UNITS + 2):
                    at(p, p)
                return
            for p in range(-1, 2):
                at(p, p)
            loop(2)
            for p in range(2 + 2 * LOOP, HEADS + 2):
                at(p, p)
            loop(HEADS + 2)
            for p in range(HEADS + 2 + 2 * LOOP, UNITS + 2):
                at(p, p)

        def head_of(p, k, batch):
            return p + (k - batch[k] * HEADS)

        def cols(ap, head, width):
            return ap[:, bass.ds(head * width, width)]

        with att, nc.Block() as block:
            @block.sync
            def _(sp):
                sp.dma_start(x_nat[:, 0:TILES, :], x[0].rearrange("(j p) d -> p j d", p=P)).then_inc(x_in[0], 16)
                sp.dma_start(wlat_raw[:], W_lat.rearrange("(c p) l -> p c l", p=P)).then_inc(wlat_in, 16)
                sp.dma_start(bias_rows[0:HEADS, :], b_d.rearrange("(h l) -> h l", l=LAT)).then_inc(bias_in, 16)
                sp.dma_start(bias_rows[B_LAT:B_LAT + 1, :], b_lat.rearrange("(a l) -> a l", a=1)).then_inc(bias_in, 16)
                sp.dma_start(bias_rows[B_ONE:B_ONE + FCH, :], b1.rearrange("(f l) -> f l", l=P)).then_inc(bias_in, 16)
                wd = W_d.rearrange("(c p) n -> p c n", p=P)
                sp.dma_start(wd_raw[:, :, 0:4 * LAT], wd[:, :, 0:4 * LAT]).then_inc(wd_in[0], 16)
                sp.dma_start(x_nat[:, TILES:2 * TILES, :], x[1].rearrange("(j p) d -> p j d", p=P)).then_inc(x_in[1], 16)
                sp.dma_start(wd_raw[:, :, 4 * LAT:], wd[:, :, 4 * LAT:]).then_inc(wd_in[1], 16)
                sp.dma_start(wp_raw[:].rearrange("l (h d) -> l h d", d=DIM), W_proj.rearrange("(h l) d -> l h d", l=LAT)).then_inc(wp_in, 16)
                for dst, src in ((bproj_all, b_proj), (b2_all, b2), (rw_all, router_w), (rb_all, router_b)):
                    n = src.shape[0]
                    sp.dma_start(dst[:], src.rearrange("(a n) -> a n", a=1).broadcast_to([P, n])).then_inc(rows_in, 16)
                sp.dma_start(wf_raw[:, 0:W2_AT].rearrange("p (c f) -> p c f", c=CH),
                             w1.rearrange("(c p) f -> p c f", p=P)).then_inc(w1_in, 16)
                sp.dma_start(wf_raw[:, W2_AT:].rearrange("p (f d) -> p f d", f=FCH),
                             w2.rearrange("(f p) d -> p f d", p=P)).then_inc(w2_in, 16)

            @block.tensor
            def _(pe):
                def product(dst, left, right, first=True, last=True, check=False):
                    (lh, ll), (rh, rl) = left, right
                    pe.matmul(dst, lh, rh, start=first, stop=False, skip_group_check=check)
                    pe.matmul(dst, lh, rl, start=False, stop=False, skip_group_check=check)
                    return pe.matmul(dst, ll, rh, start=False, stop=last, skip_group_check=check)

                pe.wait_ge(consts, 1)
                pe.wait_ge(bias_in, 48)
                n = HEADS + 1 + FCH
                pe.transpose(ps_out[:, 0, 0:n], bias_rows[:, :], ident[0:n, 0:n]).then_inc(prep_pe, 1)
                for b in range(BATCH):
                    pe.wait_ge(x_in[b], 16)
                    for c in range(CH):
                        dst = (ps_t0, ps_t1)[c]
                        if b:
                            pe.wait_ge(prep_dve, 7)
                        for j in range(TILES):
                            last = pe.transpose(dst[:, j * P:(j + 1) * P],
                                                x_nat[:, b * TILES + j, c * P:(c + 1) * P], ident[:, :])
                        last.then_inc(prep_pe, 1)
                    pe.wait_ge(prep_pool, 1)
                    for c in range(CH):
                        pe.wait_ge(prep_dve, 6 * b + 2 + c)
                        last = product(ps_qy[:, :], (wlat_hi[:, c, :], wlat_lo[:, c, :]),
                                       (xT_hi[b][:, c, :], xT_lo[b][:, c, :]), c == 0, c == CH - 1)
                    last.then_inc(prep_pe, 1)
                    pe.wait_ge(prep_dve, 6 * b + 4)
                    for j in range(TILES):
                        last = pe.transpose(ps_t0[:, j * P:(j + 1) * P], kT[b][:, j * P:(j + 1) * P], ident[:, :])
                    last.then_inc(prep_pe, 1)
                pe.wait_ge(consts, 5)
                pe.wait_ge(prep_dve, 13)

                def scores(p, batch):
                    b = batch[0]
                    for j in (3, 2, 1, 0):
                        n = max((j + 1) * P, MIN_N)
                        dst = {3: ps_s3[:, :], 2: ps_s2[:, 0:384], 1: ps_s10[:, MIN_N:], 0: ps_s10[:, 0:MIN_N]}[j]
                        if j == 3:
                            wait(pe, q_lo_done, p + 1)
                        if j:
                            wait(pe, exp_done, p * 4 - {3: 3, 2: 2, 1: 0}[j])
                        t = slice(j * P, (j + 1) * P)
                        product(dst, (qT_hi[:, t], qT_lo[:, t]), (kT_hi[b][:, 0:n], kT_lo[b][:, 0:n]), last=False)
                        last = pe.matmul(dst[:, t], ident_bf[:, :], mask_bf[:, :], start=False, stop=True)
                        if j != 1:
                            last.then_inc(scores_ready, 1)

                def turn(p, place, n):
                    tiles, dst, _ = turns[n]
                    s = (place + 1) % 2
                    if n == 0:
                        wait(pe, norm_act, p)
                        wait(pe, norm_dve, p)
                        wait(pe, norm_pool, p * 2)
                    wait(pe, pt_lo_done, p * 3 - (3, 4, 2)[n])
                    at = 0
                    for i in tiles:
                        for j in range(i, TILES):
                            last = pe.transpose(dst[:, at:at + P], p_tile(s, j)[:, i * P:(i + 1) * P], ident[:, :])
                            at += P
                    last.then_inc(pt_ready, 1)

                def queries(p, place, batch):
                    b, s = batch[1], (place + 1) % 2
                    wait(pe, wd_split, p + 2)
                    wait(pe, y_lo_done, p - 1)
                    for c in range(CH):
                        last = product(ps_qy[:, :], (wd_hi[s][:, c, :], wd_lo[s][:, c, :]),
                                       (xT_hi[b][:, c, :], xT_lo[b][:, c, :]), c == 0, c == CH - 1)
                    last.then_inc(q_ready, 1)

                def values(p, batch, live):
                    b = batch[-1]
                    wait(pe, pt_lo_done, p * 3)
                    wait(pe, q_lo_done, p + 2 if live else UNITS)
                    for i in range(TILES):
                        n = max((TILES - i) * P, MIN_N)
                        a = PT_OFF[i] + (TILES - i) * P - n
                        last = product(ps_qy[:, SEQ - n:], (k_hi[b][:, i, :], k_lo[b][:, i, :]),
                                       (pT_hi[:, a:a + n], pT_lo[:, a:a + n]), i == 0, i == TILES - 1)
                    last.then_inc(y_ready, 1)

                def project(p, place, batch):
                    b, s = batch[-2], place % 2
                    first, final = False, False
                    if isinstance(p, int):
                        first, final = p - 2 == b * HEADS, p - 2 == (b + 1) * HEADS - 1
                    wait(pe, wp_split, p - 1)
                    wait(pe, y_lo_done, p - 1)
                    if first and b:
                        pe.wait_ge(out_taken, b)
                    for j in range(TILES):
                        t = slice(j * P, (j + 1) * P)
                        last = product(ps_out[:, j, :], (yT_hi[:, t], yT_lo[:, t]), (wp_hi[s][:, :], wp_lo[s][:, :]),
                                       first and j % 2 == 0, final, True)
                    last.then_inc(proj_done, 1)

                def period(p, place, batch, live):
                    if live[0]:
                        scores(p, batch)
                    if live[-1]:
                        turn(p, place, 0)
                        turn(p, place, 1)
                    if live[1]:
                        queries(p, place, batch)
                    if live[-1]:
                        turn(p, place, 2)
                    if live[-2]:
                        project(p, place, batch)
                    if live[-1]:
                        values(p, batch, live[1])

                periods(pe, period)

            @block.scalar
            def _(act):
                for b in range(BATCH):
                    for c in range(CH):
                        act.wait_ge(prep_pe, 4 * b + 2 + c)
                        act.copy(xT_hi[b][:, c, :], (ps_t0, ps_t1)[c][:, :]).then_inc(prep_act, 1)
                    act.wait_ge(prep_dve, 6 * b + 4)
                    act.mul(kT_hi[b][:, :], kT[b][:, :], SCALE).then_inc(prep_act, 1)
                    act.wait_ge(prep_pe, 4 * b + 5)
                    act.copy(k_hi[b][:, :, :], ps_t0[:, :].rearrange("p (j l) -> p j l", l=LAT)).then_inc(prep_act, 1)

                def exps(p, place, js):
                    for j in js:
                        wait(act, negmax_done, p * 4 + (4 - j if j > 1 else 4))
                        act.activation(p_tile(place, j), score_bank[j], ACT.Exp, bias=negmax[:, place, j:j + 1],
                                       scale=1.0, accum_out=sums[:, place, j:j + 1]).then_inc(exp_done, 1)

                def turned(p, n):
                    wait(act, pt_ready, p * 3 - 2 + n)
                    dst = turns[n][2]
                    act.copy(pT_hi[:, dst], turns[n][1][:, 0:dst.stop - dst.start]).then_inc(pt_hi_done, 1)

                def period(p, place, batch, live):
                    if live[-2]:
                        wait(act, y_ready, p - 1)
                        wait(act, proj_done, p - 2)
                        act.copy(yT_hi[:, :], ps_qy[:, :]).then_inc(y_hi_done, 1)
                    if live[0]:
                        wait(act, pt_ready, p * 3 - 3)
                        exps(p, place, (3, 2))
                    if live[-1]:
                        wait(act, y_ready, p - 1)
                        turned(p, 0)
                    if live[0]:
                        exps(p, place, (1, 0))
                    if live[-1]:
                        turned(p, 1)
                    if live[1]:
                        wait(act, q_ready, p + 2)
                        wait(act, scores_ready, p * 3 + 3)
                        h = head_of(p, 1, batch)
                        act.activation(qT_hi[:, :], ps_qy[:, :], ACT.Identity,
                                       bias=cols(bias_cols, h, 1), scale=1.0).then_inc(q_hi_done, 1)
                    if live[-1]:
                        turned(p, 2)
                    if live[0]:
                        wait(act, rinv_done, p + 1)
                        act.mul(p_tile(place, 3), p_tile(place, 3), rinv[:, place, 3:4]).then_inc(norm_act, 1)

                act.wait_ge(prep_dve, 1)
                periods(act, period)

            @block.vector
            def _(dve):
                dve.wait_ge(prep_pe, 1)
                dve.tensor_copy(bias_cols[:, :], ps_out[:, 0, 0:HEADS + 1 + FCH]).then_inc(prep_dve, 1)
                for b in range(BATCH):
                    for c in range(CH):
                        dve.wait_ge(prep_act, 4 * b + 1 + c)
                        dve.tensor_tensor(xT_lo[b][:, c, :], (ps_t0, ps_t1)[c][:, :],
                                          xT_hi[b][:, c, :].bitcast(F32), ALU.subtract).then_inc(prep_dve, 1)
                    dve.wait_ge(prep_pe, 4 * b + 4)
                    dve.wait_ge(prep_dve, 1)
                    dve.tensor_scalar(kT[b][:, :], ps_qy[:, :], bias_cols[:, B_LAT:B_LAT + 1], None,
                                      ALU.add).then_inc(prep_dve, 1)
                    dve.wait_ge(prep_act, 4 * b + 3)
                    dve.wait_ge(prep_dve, 6 * b + 4)
                    dve.scalar_tensor_tensor(kT_lo[b][:, :], kT[b][:, :], SCALE, kT_hi[b][:, :].bitcast(F32),
                                             ALU.mult, ALU.subtract).then_inc(prep_dve, 1)
                    dve.wait_ge(rows_in, 64)
                    dve.wait_ge(x_in[b], 16)
                    dve.tensor_tensor(x1[:, b * TILES:(b + 1) * TILES, :], x_nat[:, b * TILES:(b + 1) * TILES, :],
                                      bproj_all[:, :].unsqueeze(1).broadcast_to([P, TILES, DIM]),
                                      ALU.add).then_inc(prep_dve, 1)
                    dve.wait_ge(prep_act, 4 * b + 4)
                    dve.tensor_tensor(k_lo[b][:, :, :], ps_t0[:, :].rearrange("p (j l) -> p j l", l=LAT),
                                      k_hi[b][:, :, :].bitcast(F32), ALU.subtract).then_inc(prep_dve, 1)

                def maxima(p, place, js):
                    for j in js:
                        if j:
                            wait(dve, scores_ready, p * 3 + {3: 1, 2: 2, 1: 3}[j])
                        dve.tensor_reduce(negmax[:, place, j:j + 1], score_bank[j], AX_X, ALU.max,
                                          negate=True).then_inc(negmax_done, 1)

                def turned(p, n):
                    wait(dve, pt_hi_done, p * 3 - 2 + n)
                    dst = turns[n][2]
                    dve.tensor_tensor(pT_lo[:, dst], turns[n][1][:, 0:dst.stop - dst.start],
                                      pT_hi[:, dst].bitcast(F32), ALU.subtract).then_inc(pt_lo_done, 1)

                def period(p, place, batch, live):
                    if live[-2]:
                        wait(dve, y_hi_done, p - 1)
                        dve.tensor_tensor(yT_lo[:, :], ps_qy[:, :], yT_hi[:, :].bitcast(F32),
                                          ALU.subtract).then_inc(y_lo_done, 1)
                    if live[0]:
                        maxima(p, place, (3, 2))
                    if live[-1]:
                        turned(p, 0)
                    if live[0]:
                        maxima(p, place, (1, 0))
                    if live[-1]:
                        turned(p, 1)
                    if live[1]:
                        wait(dve, q_hi_done, p + 2)
                        h = head_of(p, 1, batch)
                        dve.scalar_tensor_tensor(qT_lo[:, :], ps_qy[:, :], cols(bias_cols, h, 1),
                                                 qT_hi[:, :].bitcast(F32), ALU.add, ALU.subtract).then_inc(q_lo_done, 1)
                    if live[-1]:
                        turned(p, 2)
                    if live[0]:
                        wait(dve, exp_done, p * 4 + 4)
                        dve.reciprocal(rinv[:, place, :], sums[:, place, :]).then_inc(rinv_done, 1)
                        wait(dve, rinv_done, p + 1)
                        dve.tensor_scalar(p_tile(place, 2), p_tile(place, 2), rinv[:, place, 2:3], None,
                                          ALU.mult).then_inc(norm_dve, 1)
                    if live[-2] and isinstance(p, int) and (p - 1) % HEADS == 0:
                        b = batch[-2]
                        dve.wait_ge(proj_done, (b + 1) * HEADS)
                        r = x1[:, b * TILES:(b + 1) * TILES, :]
                        dve.tensor_tensor(r, ps_out[:, :, :], r, ALU.add).then_inc(out_taken, 1)

                periods(dve, period)

            @block.gpsimd
            def _(pool):
                pool.memset(ident[:, :], 0.0).then_inc(consts0, 1)
                pool.memset(mask_bf[:, :], 0.0).then_inc(consts0, 1)
                pool.memset(earlier[:, :], 1.0).then_inc(consts0, 1)
                pool.wait_ge(consts0, 1)
                pool.affine_select(out=ident[:, :], in_=ident[:, :], compare_op=ALU.not_equal, fill=1.0, base=0,
                                   pattern=[[-1, P]], channel_multiplier=1).then_inc(consts, 1)
                pool.wait_ge(consts0, 3)
                pool.affine_select(out=mask_bf[:, :], in_=mask_bf[:, :], compare_op=ALU.is_ge, fill=MASKED, base=0,
                                   pattern=[[-1, P]], channel_multiplier=1).then_inc(consts, 1)
                pool.wait_ge(consts, 1)
                pool.tensor_copy(ident_bf[:, :], ident[:, :]).then_inc(consts, 1)
                pool.memset(pT_hi[:, 0:P].bitcast(F32), 0.0).then_inc(consts, 1)
                pool.memset(pT_lo[:, 0:P].bitcast(F32), 0.0).then_inc(consts, 1)
                pool.wait_ge(wlat_in, 16)
                pool.tensor_copy(wlat_hi[:], wlat_raw[:]).then_inc(consts0, 1)
                pool.wait_ge(consts0, 4)
                pool.tensor_tensor(wlat_lo[:], wlat_raw[:], wlat_hi[:].bitcast(F32), ALU.subtract).then_inc(prep_pool, 1)

                def split(hi, lo, src, hi_done, split_done, number):
                    pool.tensor_copy(hi, src).then_inc(hi_done, 1)
                    wait(pool, hi_done, number + 1)
                    pool.tensor_tensor(lo, src, hi.bitcast(F32), ALU.subtract).then_inc(split_done, 1)

                def split_wd(unit, place, batch):
                    wait(pool, q_ready, unit - 1)
                    split(wd_hi[place][:], wd_lo[place][:], wd_raw[:, :, bass.ds((unit - batch * HEADS) * LAT, LAT)],
                          wd_hi_done, wd_split, unit)

                def period(p, place, batch, live):
                    if live[2]:
                        split_wd(p + 2, place, batch[2])
                    if live[-1]:
                        unit, s = p - 1, (place + 1) % 2
                        wait(pool, proj_done, unit - 1)
                        split(wp_hi[s][:], wp_lo[s][:], wp_raw[:, bass.ds((unit - batch[-1] * HEADS) * DIM, DIM)],
                              wp_hi_done, wp_split, unit)
                    if live[0]:
                        wait(pool, rinv_done, p + 1)
                        for j in (1, 0):
                            last = pool.tensor_scalar(p_tile(place, j), p_tile(place, j), rinv[:, place, j:j + 1], None,
                                                      ALU.mult)
                            last.then_inc(norm_pool, 1)
                        part = bass.ds(p * WF_PART, WF_PART)
                        split(wf_hi[:, part], wf_lo[:, part], wf_raw[:, part], wf_hi_done, wf_split, p)

                pool.wait_ge(wd_in[0], 16)
                split_wd(0, 0, 0)
                pool.wait_ge(wp_in, 16)
                pool.wait_ge(wd_in[1], 16)
                pool.wait_ge(w1_in, 16)
                pool.wait_ge(w2_in, 16)
                periods(pool, period)
                pool.wait_ge(consts0, 3)
                pool.affine_select(out=earlier[:, :], in_=earlier[:, :], compare_op=ALU.is_gt, fill=0.0,
                                   base=(TILES - 1) * P, pattern=[[-1, (2 * TILES - 1) * P]],
                                   channel_multiplier=1).then_inc(consts, 1)
                pool.iota(iota_row[:, :], pattern=[[1, KEEP]], base=0, channel_multiplier=0,
                          allow_small_or_imprecise_dtypes=True).then_inc(consts, 1)
                pool.iota(iota_col[:, :], pattern=[[P, RCH]], base=0, channel_multiplier=1,
                          allow_small_or_imprecise_dtypes=True).then_inc(consts, 1)
                pool.memset(minus_half[:, :], -0.5).then_inc(consts, 1)

        CONSTS = 9
        def sems(name):
            return [sem(f"{name}{b}") for b in range(BATCH)]

        stats_done, aggr_done, var_done, rstd_done, ln_done = (
            sems(n) for n in ("stats_done", "aggr_done", "var_done", "rstd_done", "ln_done"))
        dots_done, score_done, spread_done, row_ready = (
            sems(n) for n in ("dots_done", "score_done", "spread_done", "row_ready"))
        counted, rank_done, sel_done, selT_done = (sems(n) for n in ("counted", "rank_done", "sel_done", "selT_done"))
        exp_neg, weight_half, weight_done = (sems(n) for n in ("exp_neg", "weight_half", "weight_done"))
        x1_doubled = sems("x1_doubled")
        x1_hi_done, x1_split, gathered, xs_hi_done, xs_split = (
            sems(n) for n in ("x1_hi_done", "x1_split", "gathered", "xs_hi_done", "xs_split"))
        hidden_ready, gelu_done, h_hi_done, h_split = (
            sem(n) for n in ("hidden_ready", "gelu_done", "h_hi_done", "h_split"))
        net_ready, net_done, net_hi_done, net_split, scattered, sum_done = (
            sems(n) for n in ("net_ready", "net_done", "net_hi_done", "net_split", "scattered", "sum_done"))

        with ExitStack() as tail, nc.Block() as block:
            st = sb("st", [P, BATCH * 2, TILES, 6], F32, tail)
            mv = sb("mv", [P, BATCH * 2, TILES, 2], F32, tail)
            ve = sb("ve", [P, BATCH * 2, TILES], F32, tail)
            rstd = sb("rstd", [P, BATCH * 2, TILES], F32, tail)
            dots = sb("dots", [P, BATCH, TILES], F32, tail)
            score = sb("score", [P, BATCH, TILES], F32, tail)
            above = sb("above", [P, BATCH, TILES], F32, tail)
            same = sb("same", [P, BATCH, TILES], F32, tail)
            rank = sb("rank", [P, BATCH, TILES], F32, tail)
            e_neg = sb("e_neg", [P, BATCH, TILES], F32, tail)
            e_one = sb("e_one", [P, BATCH, TILES], F32, tail)
            weight = sb("weight", [P, BATCH, TILES], F32, tail)
            spread = sb("spread", [P, BATCH * 2, TILES, P], F32, tail)
            junk = sb("junk", [P, SEQ], F32, tail)
            junk2 = sb("junk2", [P, BATCH, TILES, DIM], F32, tail)
            x1_hi = sb("x1_hi", [P, BATCH * TILES, DIM], F32R, tail)
            x1_lo = sb("x1_lo", [P, BATCH * TILES, DIM], F32R, tail)
            sel = sb("sel", [P, BATCH * TILES, KEEP], F32R, tail)
            selT = sb("selT", [P, BATCH, RCH, SEQ], F32R, tail)
            xs_hi = sb("xs_hi", [P, CH, BATCH * KEEP], F32R, tail)
            xs_lo = sb("xs_lo", [P, CH, BATCH * KEEP], F32R, tail)
            hid = sb("hid", [P, FCH, BATCH * KEEP], F32, tail)
            hid_hi = sb("hid_hi", [P, FCH, BATCH * KEEP], F32R, tail)
            hid_lo = sb("hid_lo", [P, FCH, BATCH * KEEP], F32R, tail)
            net = sb("net", [P, BATCH, RCH, DIM], F32, tail)
            net_hi = sb("net_hi", [P, BATCH, RCH, DIM], F32R, tail)
            net_lo = sb("net_lo", [P, BATCH, RCH, DIM], F32R, tail)
            ps_gather = [ps_s3, ps_s2]
            ps_hidden = [ps_s10, ps_qy, ps_s3, ps_s2]
            ps_scatter = [[ps_t0, ps_t1], [ps_s10, ps_qy]]

            def x1_of(b):
                return x1[:, b * TILES:(b + 1) * TILES, :]

            def chosen(b):
                return slice(b * KEEP, (b + 1) * KEEP)

            @block.vector
            def _(dve):
                def layernorm(b, which):
                    k, n = which * BATCH + b, which * TILES
                    for j in range(TILES):
                        dve.bn_stats(st[:, k, j, :], x1[:, b * TILES + j, :]).then_inc(stats_done[b], 1)
                    for j in range(TILES):
                        dve.wait_ge(stats_done[b], n + j + 1)
                        dve.bn_aggr(mv[:, k, j, :], st[:, k, j, :]).then_inc(aggr_done[b], 1)
                    dve.wait_ge(aggr_done[b], n + TILES)
                    dve.tensor_scalar(ve[:, k, :], mv[:, k, :, 1], EPS, None, ALU.add).then_inc(var_done[b], 1)
                    dve.wait_ge(rstd_done[b], which + 1)
                    for j in range(TILES):
                        r = x1[:, b * TILES + j, :]
                        dve.tensor_scalar(r, r, mv[:, k, j, 0:1], rstd[:, k, j:j + 1],
                                          ALU.subtract, ALU.mult).then_inc(ln_done[b], 1)

                def router_scores(b):
                    for j in range(TILES):
                        dve.wait_ge(ln_done[b], j + 1)
                        dve.scalar_tensor_tensor(junk2[:, b, j, :], x1[:, b * TILES + j, :], 1.0, rw_all[:, :], ALU.mult,
                                                 ALU.mult, accum_out=dots[:, b, j:j + 1]).then_inc(dots_done[b], 1)
                    dve.wait_ge(dots_done[b], TILES)
                    dve.tensor_scalar(score[:, b, :], dots[:, b, :], rb_all[:, 0:1], None, ALU.add).then_inc(score_done[b], 1)
                    dve.wait_ge(score_done[b], 1)
                    dve.tensor_copy(spread[:, b, :, :], score[:, b, :].unsqueeze(2).broadcast_to([P, TILES, P])
                                    ).then_inc(spread_done[b], 1)

                def ranks(b):
                    dve.wait_ge(row_ready[b], 1)
                    for j in range(TILES):
                        mine = score[:, b, j:j + 1]
                        before = earlier[:, (TILES - 1 - j) * P:(TILES - 1 - j) * P + SEQ]
                        dve.tensor_scalar(junk[:, :], ps_t0[:, :], mine, None, ALU.is_gt, ALU.add,
                                          accum_out=above[:, b, j:j + 1]).then_inc(counted[b], 1)
                        dve.wait_ge(counted[b], 2 * j + 1)
                        dve.scalar_tensor_tensor(junk[:, :], ps_t0[:, :], mine, before, ALU.is_equal, ALU.mult,
                                                 accum_out=same[:, b, j:j + 1]).then_inc(counted[b], 1)
                        dve.wait_ge(counted[b], 2 * j + 2)
                    dve.tensor_tensor(rank[:, b, :], above[:, b, :], same[:, b, :], ALU.add).then_inc(rank_done[b], 1)
                    dve.wait_ge(rank_done[b], 1)
                    dve.tensor_copy(spread[:, BATCH + b, :, :], rank[:, b, :].unsqueeze(2).broadcast_to([P, TILES, P])
                                    ).then_inc(spread_done[b], 1)
                    for j in range(TILES):
                        dve.tensor_scalar(sel[:, b * TILES + j, :], iota_row[:, :], rank[:, b, j:j + 1], None,
                                          ALU.is_equal).then_inc(sel_done[b], 1)
                    dve.wait_ge(row_ready[b], 2)
                    for q in range(RCH):
                        dve.tensor_scalar(selT[:, b, q, :], ps_t1[:, :], iota_col[:, q:q + 1], None,
                                          ALU.is_equal).then_inc(selT_done[b], 1)
                    dve.wait_ge(exp_neg[b], 1)
                    dve.tensor_scalar(e_one[:, b, :], e_neg[:, b, :], 1.0, None, ALU.add).then_inc(weight_half[b], 1)
                    dve.wait_ge(weight_half[b], 1)
                    dve.reciprocal(weight[:, b, :], e_one[:, b, :]).then_inc(weight_done[b], 1)

                dve.wait_ge(rows_in, 64)
                dve.wait_ge(consts, CONSTS)
                for b in range(BATCH):
                    dve.wait_ge(out_taken, b + 1)
                    layernorm(b, 0)
                    router_scores(b)
                    ranks(b)
                    for c in range(CH):
                        dve.wait_ge(xs_hi_done[b], c + 1)
                        dve.tensor_tensor(xs_lo[:, c, chosen(b)], ps_gather[c][:, chosen(b)],
                                          xs_hi[:, c, chosen(b)].bitcast(F32), ALU.subtract).then_inc(xs_split[b], 1)
                for f in range(FCH):
                    dve.wait_ge(gelu_done, f + 1)
                    dve.tensor_copy(hid_hi[:, f, :], hid[:, f, :]).then_inc(h_hi_done, 1)
                    dve.wait_ge(h_hi_done, f + 1)
                    dve.tensor_tensor(hid_lo[:, f, :], hid[:, f, :], hid_hi[:, f, :].bitcast(F32),
                                      ALU.subtract).then_inc(h_split, 1)
                for b in range(BATCH):
                    dve.wait_ge(net_ready[b], 1)
                    dve.tensor_tensor(net[:, b, :, :], ps_out[:, b * RCH:(b + 1) * RCH, :],
                                      b2_all[:, :].unsqueeze(1).broadcast_to([P, RCH, DIM]), ALU.add).then_inc(net_done[b], 1)
                    dve.wait_ge(net_hi_done[b], 1)
                    dve.tensor_tensor(net_lo[:, b, :, :], net[:, b, :, :], net_hi[:, b, :, :].bitcast(F32),
                                      ALU.subtract).then_inc(net_split[b], 1)
                for b in range(BATCH):
                    dve.wait_ge(weight_done[b], 1)
                    dve.wait_ge(x1_doubled[b], 1)
                    for j in range(TILES):
                        r = x1[:, b * TILES + j, :]
                        dve.wait_ge(scattered[b], j // 2 + 1)
                        dve.scalar_tensor_tensor(r, ps_scatter[b][j // 2][:, (j % 2) * DIM:(j % 2 + 1) * DIM],
                                                 weight[:, b, j:j + 1], r, ALU.mult, ALU.add).then_inc(sum_done[b], 1)
                    dve.wait_ge(sum_done[b], TILES)
                    layernorm(b, 1)

            @block.gpsimd
            def _(pool):
                for which in range(2):
                    for b in range(BATCH):
                        k = which * BATCH + b
                        pool.wait_ge(var_done[b], which + 1)
                        pool.tensor_tensor(rstd[:, k, :], ve[:, k, :], minus_half[:, :], ALU.pow).then_inc(rstd_done[b], 1)
                        if which == 0:
                            pool.wait_ge(x1_hi_done[b], 1)
                            pool.tensor_tensor(x1_lo[:, b * TILES:(b + 1) * TILES, :], x1_of(b),
                                               x1_hi[:, b * TILES:(b + 1) * TILES, :].bitcast(F32),
                                               ALU.subtract).then_inc(x1_split[b], 1)

            @block.scalar
            def _(act):
                for b in range(BATCH):
                    act.wait_ge(ln_done[b], TILES)
                    act.copy(x1_hi[:, b * TILES:(b + 1) * TILES, :], x1_of(b)).then_inc(x1_hi_done[b], 1)
                    act.wait_ge(score_done[b], 1)
                    act.activation(e_neg[:, b, :], score[:, b, :], ACT.Exp, bias=0.0, scale=-1.0).then_inc(exp_neg[b], 1)
                    act.wait_ge(x1_split[b], 1)
                    act.wait_ge(dots_done[b], TILES)
                    act.mul(x1_of(b), x1_of(b), 2.0).then_inc(x1_doubled[b], 1)
                    act.wait_ge(gathered[b], 1)
                    for c in range(CH):
                        act.copy(xs_hi[:, c, chosen(b)], ps_gather[c][:, chosen(b)]).then_inc(xs_hi_done[b], 1)
                for f in range(FCH):
                    act.wait_ge(hidden_ready, f + 1)
                    act.activation(hid[:, f, :], ps_hidden[f % 4][:, :], ACT.Gelu_apprx_tanh,
                                   bias=bias_cols[:, B_ONE + f:B_ONE + f + 1], scale=1.0).then_inc(gelu_done, 1)
                for b in range(BATCH):
                    act.wait_ge(net_done[b], 1)
                    act.copy(net_hi[:, b, :, :], net[:, b, :, :]).then_inc(net_hi_done[b], 1)

            @block.tensor
            def _(pe):
                def product(dst, left, right, first=True, last=True, check=False):
                    (lh, ll), (rh, rl) = left, right
                    pe.matmul(dst, lh, rh, start=first, stop=False, skip_group_check=check)
                    pe.matmul(dst, lh, rl, start=False, stop=False, skip_group_check=check)
                    return pe.matmul(dst, ll, rh, start=False, stop=last, skip_group_check=check)

                for b in range(BATCH):
                    for k, dst in ((b, ps_t0), (BATCH + b, ps_t1)):
                        pe.wait_ge(spread_done[b], k // BATCH + 1)
                        for j in range(TILES):
                            last = pe.transpose(dst[:, j * P:(j + 1) * P], spread[:, k, j, :], ident[:, :])
                        last.then_inc(row_ready[b], 1)
                    pe.wait_ge(sel_done[b], TILES)
                    pe.wait_ge(x1_split[b], 1)
                    for c in range(CH):
                        for j in range(TILES):
                            t, cols_c = b * TILES + j, slice(c * P, (c + 1) * P)
                            pe.matmul(ps_gather[c][:, chosen(b)], x1_hi[:, t, cols_c], sel[:, t, :],
                                      start=(j == 0), stop=False)
                            last = pe.matmul(ps_gather[c][:, chosen(b)], x1_lo[:, t, cols_c], sel[:, t, :],
                                             start=False, stop=(j == TILES - 1))
                    last.then_inc(gathered[b], 1)
                for b in range(BATCH):
                    pe.wait_ge(xs_split[b], CH)
                pe.wait_ge(wf_split, UNITS)
                for f in range(FCH):
                    if f >= 4:
                        pe.wait_ge(gelu_done, f - 3)
                    for c in range(CH):
                        w = slice(c * FFN + f * P, c * FFN + (f + 1) * P)
                        last = product(ps_hidden[f % 4][:, :], (wf_hi[:, w], wf_lo[:, w]),
                                       (xs_hi[:, c, :], xs_lo[:, c, :]), c == 0, c == CH - 1)
                    last.then_inc(hidden_ready, 1)
                for f in range(FCH):
                    pe.wait_ge(h_split, f + 1)
                    w = slice(W2_AT + f * DIM, W2_AT + (f + 1) * DIM)
                    for r in range(BATCH * RCH):
                        t = slice(r * P, (r + 1) * P)
                        last = product(ps_out[:, r, :], (hid_hi[:, f, t], hid_lo[:, f, t]), (wf_hi[:, w], wf_lo[:, w]),
                                       f == 0 and r % RCH == 0, f == FCH - 1, True)
                        if f == FCH - 1 and r % RCH == RCH - 1:
                            last.then_inc(net_ready[r // RCH], 1)
                for b in range(BATCH):
                    pe.wait_ge(net_split[b], 1)
                    pe.wait_ge(selT_done[BATCH - 1], RCH)
                    for j in range(TILES):
                        dst = ps_scatter[b][j // 2][:, (j % 2) * DIM:(j % 2 + 1) * DIM]
                        for q in range(RCH):
                            one = selT[:, b, q, j * P:(j + 1) * P]
                            pe.matmul(dst, one, net_hi[:, b, q, :], start=(q == 0), stop=False)
                            last = pe.matmul(dst, one, net_lo[:, b, q, :], start=False, stop=(q == RCH - 1))
                        if j % 2:
                            last.then_inc(scattered[b], 1)

            @block.sync
            def _(sp):
                for b in range(BATCH):
                    sp.wait_ge(ln_done[b], 2 * TILES)
                    sp.dma_start(out[b].rearrange("(j p) d -> p j d", p=P), x1_of(b)).then_inc(stored[b], 16)
                for b in range(BATCH):
                    sp.wait_ge(stored[b], 16)
    return nc


_INS = ["L0_attn_x", "L0_attn_W_lat", "L0_attn_b_lat", "L0_attn_W_d", "L0_attn_b_d", "L0_attn_W_proj",
        "L0_attn_b_proj", "L0_ffn_router_weight", "L0_ffn_router_bias", "L0_ffn_w1", "L0_ffn_b1",
        "L0_ffn_w2", "L0_ffn_b2"]


def kernel(**inputs):
    import numpy as np
    from concourse import bacc
    from concourse.bass_utils import run_bass_kernel_spmd

    nc = bacc.Bacc("TRN2", target_bir_lowering=False, num_devices=1)
    arrays, args = {}, []
    for name in _INS:
        a = np.ascontiguousarray(inputs[name])
        arrays[f"in_{name}"] = a
        args.append(nc.dram_tensor(f"in_{name}", a.shape, mybir.dt.from_np(a.dtype), kind="ExternalInput").ap())
    out = nc.dram_tensor("out", (BATCH, SEQ, DIM), F32, kind="ExternalOutput").ap()
    mk_layer_kernel(nc, *args, out)
    r = run_bass_kernel_spmd(nc, [arrays], core_ids=[0])
    return r.results[0]["out"]
```

```python
import math
from contextlib import ExitStack

import concourse.bass as bass
from concourse import mybir

F32 = mybir.dt.float32
F32R = mybir.dt.float32r
BF16 = mybir.dt.bfloat16
ACT = mybir.ActivationFunctionType
ALU = mybir.AluOpType
AX_X = mybir.AxisListType.X

P = 128
BATCH, SEQ, DIM = 2, 512, 256
HEADS, LAT = 16, 128
FFN = 1024
KEEP = SEQ // 2
TILES = SEQ // P
CH = DIM // P
FCH = FFN // P
RCH = KEEP // P
UNITS = BATCH * HEADS
SCALE = 1.0 / math.sqrt(LAT)
EPS = 1e-5
MASKED = -1.0e38
MIN_N = 256

P_OFF = [P * (j * (j + 1) // 2) for j in range(TILES)]
P_COLS = P * TILES * (TILES + 1) // 2
PT_OFF = {3: P, 2: 2 * P, 1: 4 * P, 0: 7 * P}
PT_COLS = 11 * P


def mk_layer_kernel(nc, x, W_lat, b_lat, W_d, b_d, W_proj, b_proj, router_w, router_b,
                    w1, b1, w2, b2, out):
    with ExitStack() as top:
        def sb(name, shape, dt=F32, stack=top):
            return stack.enter_context(nc.sbuf_tensor(name, shape, dt))

        def sem(name):
            return top.enter_context(nc.semaphore(name))

        x1 = sb("x1", [P, BATCH * TILES, DIM])
        W2_AT = CH * FFN
        WF_COLS = W2_AT + FCH * DIM
        wf_raw = sb("wf_raw", [P, WF_COLS])
        wf_hi, wf_lo = (sb(n, [P, WF_COLS], F32R) for n in ("wf_hi", "wf_lo"))
        ident = sb("ident", [P, P])
        ident_bf = sb("ident_bf", [P, P], BF16)
        ones_bf = sb("ones_bf", [P, P], BF16)
        mask_bf = sb("mask_bf", [P, P], BF16)
        earlier = sb("earlier", [P, P], BF16)
        iota_row = sb("iota_row", [P, KEEP])
        iota_col = sb("iota_col", [P, RCH])
        bias_rows = sb("bias_rows", [HEADS + 1 + FCH, P])
        bias_cols = sb("bias_cols", [P, HEADS + 1 + FCH])
        bproj_all = sb("bproj_all", [P, DIM])
        b2_all = sb("b2_all", [P, DIM])
        rw_all = sb("rw_all", [P, DIM])
        rb_all = sb("rb_all", [P, 1])
        zero = sb("zero", [P, 512])
        minus_half = sb("minus_half", [P, TILES])
        negmax = sb("negmax", [P, 2, TILES])
        sums = sb("sums", [P, 2, TILES])
        rinv = sb("rinv", [P, 2, TILES])
        B_LAT = HEADS
        B_ONE = HEADS + 1
        st = sb("st", [P, BATCH * 2, TILES, 6])
        mv = sb("mv", [P, BATCH * 2, TILES, 2])
        ve = sb("ve", [P, BATCH * 2, TILES])
        rstd = sb("rstd", [P, BATCH * 2, TILES])
        dots = sb("dots", [P, BATCH, TILES])
        score = sb("score", [P, BATCH, TILES])
        score_row = sb("score_row", [P, SEQ])
        beats = sb("beats", [P, TILES, SEQ], BF16)
        ties = sb("ties", [P, TILES, P], BF16)
        rank_row = sb("rank_row", [P, SEQ])
        rank = sb("rank", [P, TILES])
        e_neg = sb("e_neg", [P, BATCH, TILES])
        e_one = sb("e_one", [P, BATCH, TILES])
        weight = sb("weight", [P, BATCH, TILES])
        x1_hi = sb("x1_hi", [P, BATCH * TILES, DIM], F32R)
        x1_lo = sb("x1_lo", [P, BATCH * TILES, DIM], F32R)
        sel = sb("sel", [P, BATCH * TILES, KEEP], F32R)
        selT = sb("selT", [P, BATCH, RCH, SEQ], F32R)

        bank = [top.enter_context(nc.psum_tensor(f"bank{i}", [P, 512], F32)) for i in range(6)]
        ps_s3, ps_s2, ps_s10, ps_t0, ps_t1, ps_qy = bank
        ps_out = top.enter_context(nc.psum_tensor("ps_out", [P, TILES, DIM], F32))

        def sems(name):
            return [sem(f"{name}{b}") for b in range(BATCH)]

        x_in, wd_in, wp_in = sems("x_in"), sems("wd_in"), sems("wp_in")
        wlat_in, bias_in, rows_in, w1_in, w2_in = (sem(n) for n in ("wlat_in", "bias_in", "rows_in", "w1_in", "w2_in"))
        filled, ident_done, consts = sem("filled"), sem("ident_done"), sem("consts")
        bias_turned, bias_done = sem("bias_turned"), sem("bias_done")
        wlat_hi_done, wlat_split = sem("wlat_hi_done"), sem("wlat_split")
        x_turned, x_hi_done, x_split, x1_started = sem("x_turned"), sem("x_hi_done"), sem("x_split"), sem("x1_started")
        kT_ready, kT_done, kT_hi_done, kT_split = sem("kT_ready"), sem("kT_done"), sem("kT_hi_done"), sem("kT_split")
        k_turned, k_hi_done, k_split = sem("k_turned"), sem("k_hi_done"), sem("k_split")
        wd_hi_done, wd_split = sem("wd_hi_done"), sem("wd_split")
        wp_hi_done, wp_split = sem("wp_hi_done"), sem("wp_split")
        wf_hi_done, wf_split = sem("wf_hi_done"), sem("wf_split")
        q_ready, q_hi_done, q_lo_done = sem("q_ready"), sem("q_hi_done"), sem("q_lo_done")
        scores_ready, negmax_done, exp_done, rinv_done = (
            sem(n) for n in ("scores_ready", "negmax_done", "exp_done", "rinv_done"))
        norm_act, norm_dve = sem("norm_act"), sem("norm_dve")
        pt_ready, pt_hi_done, pt_lo_done = sem("pt_ready"), sem("pt_hi_done"), sem("pt_lo_done")
        y_ready, y_hi_done, y_lo_done = sem("y_ready"), sem("y_hi_done"), sem("y_lo_done")
        proj_done, out_taken = sem("proj_done"), sem("out_taken")
        stats_done, aggr_done, var_done, rstd_done, ln_done = (
            sems(n) for n in ("stats_done", "aggr_done", "var_done", "rstd_done", "ln_done"))
        dots_done, score_done, score_turned, score_row_done = (
            sems(n) for n in ("dots_done", "score_done", "score_turned", "score_row_done"))
        compared, rank_row_ready, rank_ready, rank_row_done, rank_done = (
            sems(n) for n in ("compared", "rank_row_ready", "rank_ready", "rank_row_done", "rank_done"))
        sel_done, selT_done, exp_neg, weight_half, weight_done = (
            sems(n) for n in ("sel_done", "selT_done", "exp_neg", "weight_half", "weight_done"))
        x1_hi_done, x1_split, x1_doubled = sems("x1_hi_done"), sems("x1_split"), sems("x1_doubled")
        gathered, xs_hi_done, xs_split = sems("gathered"), sems("xs_hi_done"), sems("xs_split")
        hid_ready, gelu_done, hid_hi_done, hid_split = (
            sems(n) for n in ("hid_ready", "gelu_done", "hid_hi_done", "hid_split"))
        net_ready, net_done, net_hi_done, net_split = (
            sems(n) for n in ("net_ready", "net_done", "net_hi_done", "net_split"))
        scattered, sum_done, stored = sems("scattered"), sems("sum_done"), sems("stored")

        def wait(eng, s, value):
            if not isinstance(value, int) or value > 0:
                eng.wait_ge(s, value)

        att = ExitStack()
        x_nat = sb("x_nat", [P, BATCH * TILES, DIM], F32, att)
        wlat_raw = sb("wlat_raw", [P, CH, LAT], F32, att)
        wlat_hi, wlat_lo = sb("wlat_hi", [P, CH, LAT], F32R, att), sb("wlat_lo", [P, CH, LAT], F32R, att)
        xT_hi = [sb(f"xT_hi{b}", [P, CH, SEQ], F32R, att) for b in range(BATCH)]
        xT_lo = [sb(f"xT_lo{b}", [P, CH, SEQ], F32R, att) for b in range(BATCH)]
        kT = [sb(f"kT{b}", [P, SEQ], F32, att) for b in range(BATCH)]
        kT_hi = [sb(f"kT_hi{b}", [P, SEQ], F32R, att) for b in range(BATCH)]
        kT_lo = [sb(f"kT_lo{b}", [P, SEQ], F32R, att) for b in range(BATCH)]
        k_hi = [sb(f"k_hi{b}", [P, TILES, LAT], F32R, att) for b in range(BATCH)]
        k_lo = [sb(f"k_lo{b}", [P, TILES, LAT], F32R, att) for b in range(BATCH)]
        wd_raw = [sb(f"wd_raw{s}", [P, CH, LAT], F32, att) for s in range(2)]
        wd_hi = [sb(f"wd_hi{s}", [P, CH, LAT], F32R, att) for s in range(2)]
        wd_lo = [sb(f"wd_lo{s}", [P, CH, LAT], F32R, att) for s in range(2)]
        wp_raw = [sb(f"wp_raw{s}", [P, DIM], F32, att) for s in range(2)]
        wp_hi = [sb(f"wp_hi{s}", [P, DIM], F32R, att) for s in range(2)]
        wp_lo = [sb(f"wp_lo{s}", [P, DIM], F32R, att) for s in range(2)]
        qT_hi, qT_lo = sb("qT_hi", [P, SEQ], F32R, att), sb("qT_lo", [P, SEQ], F32R, att)
        yT_hi, yT_lo = sb("yT_hi", [P, SEQ], F32R, att), sb("yT_lo", [P, SEQ], F32R, att)
        probs = [sb(f"probs{s}", [P, P_COLS], F32, att) for s in range(2)]
        pT_hi, pT_lo = sb("pT_hi", [P, PT_COLS], F32R, att), sb("pT_lo", [P, PT_COLS], F32R, att)
        att.close()
        xs_hi = sb("xs_hi", [P, BATCH, CH, KEEP], F32R)
        xs_lo = sb("xs_lo", [P, BATCH, CH, KEEP], F32R)
        hid = sb("hid", [P, FCH, KEEP])
        hid_hi = sb("hid_hi", [P, BATCH, FCH, KEEP], F32R)
        hid_lo = sb("hid_lo", [P, BATCH, FCH, KEEP], F32R)
        net = sb("net", [P, BATCH, RCH, DIM])
        net_hi = sb("net_hi", [P, BATCH, RCH, DIM], F32R)
        net_lo = sb("net_lo", [P, BATCH, RCH, DIM], F32R)

        def p_tile(s, j):
            return probs[s][:, P_OFF[j]:P_OFF[j] + (j + 1) * P]

        score_bank = {3: ps_s3[:, :], 2: ps_s2[:, 0:384], 1: ps_s10[:, MIN_N:2 * MIN_N], 0: ps_s10[:, 0:P]}

        turns = [([0], ps_t0, slice(PT_OFF[0], PT_OFF[0] + 4 * P)),
                 ([1], ps_t1, slice(PT_OFF[1], PT_OFF[1] + 3 * P)),
                 ([3, 2], ps_t0, slice(PT_OFF[3], PT_OFF[3] + 3 * P))]

        class Period:

            def __init__(self, p, fixed, turn):
                self.p, self.fixed, self.turn = p, fixed, turn

            def live(self, k):
                return 0 <= self.fixed + k < UNITS

            def batch(self, k):
                return (self.fixed + k) // HEADS

            def place(self, k):
                return (self.fixed + k) % 2

            def use(self, k):
                return self.turn + (self.fixed + k) // 2

            def head(self, k):
                return self.p + (k - self.batch(k) * HEADS)

        LOOPS = [(3, 5), (24, 2)]
        LAST = UNITS + 2

        def periods(eng, body):
            p = -1
            for first, times in LOOPS + [(LAST, 0)]:
                for q in range(p, first):
                    body(Period(q, q, 0))
                if times:
                    with eng.Fori(0, times) as i:
                        for q in range(first, first + 2):
                            body(Period(i * 2 + q, q, i))
                p = first + 2 * times

        CONSTS = 9
        AT_STATS, AT_APPLY, AT_TURN, AT_COMPARE, AT_RANK_ROW, AT_RANK, AT_SELECT = 18, 19, 20, 21, 21, 22, 23
        WF_PERIODS = [13, 14, 15, 16, 17, 18, 21, 22]
        WF_PART = WF_COLS // len(WF_PERIODS)

        def x1_of(b):
            return x1[:, b * TILES:(b + 1) * TILES, :]

        def hidden_bank(b, f):
            return (ps_s10, ps_qy, ps_s2, ps_s10)[f // 2][:, (f % 2) * KEEP:(f % 2 + 1) * KEEP]

        def net_bank(b, r):
            return ps_out[:, 2 * r + b, :]

        block = top.enter_context(nc.Block())

        @block.sync
        def _(sp):
            wd = W_d.rearrange("(c p) n -> p c n", p=P)

            def load_wd(unit, place, head, batch):
                wait(sp, wd_split, unit - 1)
                sp.dma_start(wd_raw[place][:], wd[:, :, bass.ds(head * LAT, LAT)]).then_inc(wd_in[place], 16)

            def load_wp(unit, place, head):
                wait(sp, wp_split, unit - 1)
                sp.dma_start(wp_raw[place][:], W_proj[bass.ds(head * LAT, LAT), :]).then_inc(wp_in[place], 16)

            for j in range(0, TILES, 2):
                sp.dma_start(x_nat[:, j:j + 2, :], x[0, j * P:(j + 2) * P].rearrange("(j p) d -> p j d", p=P)).then_inc(x_in[0], 16)
            sp.dma_start(wlat_raw[:], W_lat.rearrange("(c p) l -> p c l", p=P)).then_inc(wlat_in, 16)
            sp.dma_start(bias_rows[0:HEADS, :], b_d.rearrange("(h l) -> h l", l=LAT)).then_inc(bias_in, 16)
            sp.dma_start(bias_rows[B_LAT:B_LAT + 1, :], b_lat.rearrange("(a l) -> a l", a=1)).then_inc(bias_in, 16)
            sp.dma_start(bias_rows[B_ONE:B_ONE + FCH, :], b1.rearrange("(f l) -> f l", l=P)).then_inc(bias_in, 16)
            for u in range(2):
                load_wd(u, u, u, 0)
            sp.dma_start(x_nat[:, TILES:2 * TILES, :], x[1].rearrange("(j p) d -> p j d", p=P)).then_inc(x_in[1], 16)
            load_wp(0, 0, 0)
            for dst, src in ((bproj_all, b_proj), (b2_all, b2), (rw_all, router_w), (rb_all, router_b)):
                n = src.shape[0]
                sp.dma_start(dst[:], src.rearrange("(a n) -> a n", a=1).broadcast_to([P, n])).then_inc(rows_in, 16)

            def period(at):
                if at.live(3) and at.fixed >= -1:
                    load_wd(at.p + 3, at.place(3), at.head(3), at.batch(3))
                if at.live(0) and at.fixed >= 1:
                    load_wp(at.p, at.place(0), at.head(0))
                if at.fixed == 1:
                    sp.dma_start(wf_raw[:, 0:W2_AT].rearrange("p (c f) -> p c f", c=CH),
                                 w1.rearrange("(c p) f -> p c f", p=P)).then_inc(w1_in, 16)
                    sp.dma_start(wf_raw[:, W2_AT:].rearrange("p (f d) -> p f d", f=FCH),
                                 w2.rearrange("(f p) d -> p f d", p=P)).then_inc(w2_in, 16)

            periods(sp, period)
            for b in range(BATCH):
                for half in range(2):
                    sp.wait_ge(ln_done[b], TILES + 2 * (half + 1))
                    sp.dma_start(out[b, half * 2 * P:(half + 1) * 2 * P].rearrange("(j p) d -> p j d", p=P),
                                 x1[:, b * TILES + 2 * half:b * TILES + 2 * half + 2, :]).then_inc(stored[b], 16)
            for b in range(BATCH):
                sp.wait_ge(stored[b], 32)

        @block.tensor
        def _(pe):
            def product(dst, left, right, first=True, last=True, check=False):
                (lh, ll), (rh, rl) = left, right
                pe.matmul(dst, lh, rh, start=first, stop=False, skip_group_check=check)
                pe.matmul(dst, lh, rl, start=False, stop=False, skip_group_check=check)
                return pe.matmul(dst, ll, rh, start=False, stop=last, skip_group_check=check)

            pe.wait_ge(ident_done, 1)
            for b in range(BATCH):
                pe.wait_ge(x_in[b], 32 if b == 0 else 16)
                if b:
                    pe.wait_ge(k_split, 1)
                for c in range(CH):
                    dst = (ps_t0, ps_t1)[c]
                    for j in range(TILES):
                        last = pe.transpose(dst[:, j * P:(j + 1) * P],
                                            x_nat[:, b * TILES + j, c * P:(c + 1) * P], ident[:, :])
                    last.then_inc(x_turned, 1)
                if b == 0:
                    pe.wait_ge(bias_in, 48)
                    n = HEADS + 1 + FCH
                    pe.transpose(ps_out[:, 0, 0:n], bias_rows[:, :], ident[0:n, 0:n]).then_inc(bias_turned, 1)
                pe.wait_ge(wlat_split, 1)
                if b:
                    pe.wait_ge(q_lo_done, 1)
                for c in range(CH):
                    pe.wait_ge(x_split, CH * b + c + 1)
                    last = product(ps_qy[:, :], (wlat_hi[:, c, :], wlat_lo[:, c, :]),
                                   (xT_hi[b][:, c, :], xT_lo[b][:, c, :]), c == 0, c == CH - 1)
                last.then_inc(kT_ready, 1)
                pe.wait_ge(kT_done, b + 1)
                for j in range(TILES):
                    last = pe.transpose(ps_t0[:, j * P:(j + 1) * P], kT[b][:, j * P:(j + 1) * P], ident[:, :])
                last.then_inc(k_turned, 1)
                if b == 0:
                    pe.wait_ge(wd_split, 1)
                    for c in range(CH):
                        last = product(ps_qy[:, :], (wd_hi[0][:, c, :], wd_lo[0][:, c, :]),
                                       (xT_hi[0][:, c, :], xT_lo[0][:, c, :]), c == 0, c == CH - 1)
                    last.then_inc(q_ready, 1)
            pe.wait_ge(consts, 5)
            pe.wait_ge(kT_split, 2)
            pe.wait_ge(k_split, 2)

            def scores(at):
                p, b = at.p, at.batch(0)
                for j in (3, 2, 1, 0):
                    n = max((j + 1) * P, MIN_N)
                    dst = {3: ps_s3[:, :], 2: ps_s2[:, 0:384], 1: ps_s10[:, MIN_N:], 0: ps_s10[:, 0:MIN_N]}[j]
                    if j == 3:
                        wait(pe, q_lo_done, p + 1)
                    if j:
                        wait(pe, exp_done, p * 4 - {3: 3, 2: 2, 1: 0}[j])
                    t = slice(j * P, (j + 1) * P)
                    product(dst, (qT_hi[:, t], qT_lo[:, t]), (kT_hi[b][:, 0:n], kT_lo[b][:, 0:n]), last=False)
                    last = pe.matmul(dst[:, t], ident_bf[:, :], mask_bf[:, :], start=False, stop=True)
                    if j != 1:
                        last.then_inc(scores_ready, 1)

            def turn(at, n):
                p, s = at.p, at.place(-1)
                tiles, dst, _ = turns[n]
                if n == 0:
                    wait(pe, norm_act, p)
                    wait(pe, norm_dve, p * 3)
                wait(pe, pt_lo_done, p * 3 - (3, 4, 2)[n])
                if n == 1 and at.fixed - 1 in (AT_TURN, AT_RANK_ROW, AT_RANK):
                    pe.wait_ge({AT_TURN: score_row_done, AT_RANK_ROW: rank_row_done, AT_RANK: rank_done}[at.fixed - 1][0], 1)
                a = 0
                for i in tiles:
                    for j in range(i, TILES):
                        last = pe.transpose(dst[:, a:a + P], p_tile(s, j)[:, i * P:(i + 1) * P], ident[:, :])
                        a += P
                last.then_inc(pt_ready, 1)

            def queries(at):
                b, s = at.batch(1), at.place(1)
                wait(pe, wd_split, at.p + 2)
                wait(pe, y_lo_done, at.p - 1)
                for c in range(CH):
                    last = product(ps_qy[:, :], (wd_hi[s][:, c, :], wd_lo[s][:, c, :]),
                                   (xT_hi[b][:, c, :], xT_lo[b][:, c, :]), c == 0, c == CH - 1)
                last.then_inc(q_ready, 1)

            def project(at):
                b, s = at.batch(-2), at.place(-2)
                head = at.fixed - 2 - b * HEADS
                wait(pe, wp_split, at.p - 1)
                wait(pe, y_lo_done, at.p - 1)
                if head == 0 and b:
                    pe.wait_ge(out_taken, b)
                for j in range(TILES):
                    t = slice(j * P, (j + 1) * P)
                    last = product(ps_out[:, j, :], (yT_hi[:, t], yT_lo[:, t]), (wp_hi[s][:, :], wp_lo[s][:, :]),
                                   head == 0 and j % 2 == 0, head == HEADS - 1, True)
                last.then_inc(proj_done, 1)

            def values(at):
                p, b = at.p, at.batch(-1)
                wait(pe, q_lo_done, p + 2 if at.live(1) else UNITS)
                for i, ready in ((0, 1), (1, 2), (2, 3), (3, 3)):
                    if i < 3:
                        wait(pe, pt_lo_done, p * 3 - 3 + ready)
                    n = max((TILES - i) * P, MIN_N)
                    a = PT_OFF[i] + (TILES - i) * P - n
                    last = product(ps_qy[:, SEQ - n:], (k_hi[b][:, i, :], k_lo[b][:, i, :]),
                                   (pT_hi[:, a:a + n], pT_lo[:, a:a + n]), i == 0, i == TILES - 1)
                last.then_inc(y_ready, 1)

            def turn_scores(b, dst):
                pe.wait_ge(score_done[b], 1)
                for j in range(TILES):
                    last = pe.transpose(dst[:, j * P:(j + 1) * P], score[:, b, j:j + 1].to_broadcast([P, P]), ident[:, :])
                last.then_inc(score_turned[b], 1)

            def rank_rows(b, dst):
                pe.wait_ge(compared[b], 3 * TILES - 1)
                for j in range(TILES):
                    pe.matmul(dst[:, :], ones_bf[:, :], beats[:, j, :], start=(j == 0), stop=False)
                for j in range(TILES):
                    last = pe.matmul(dst[:, j * P:(j + 1) * P], ones_bf[:, :], ties[:, j, :], start=False,
                                     stop=(j == TILES - 1))
                last.then_inc(rank_row_ready[b], 1)

            def rank_cols(b, dst):
                for j in range(TILES):
                    for i in range(TILES):
                        pe.matmul(dst[:, j:j + 1], beats[:, i, j * P:(j + 1) * P], ones_bf[:, 0:1],
                                  start=(i == 0), stop=False)
                    last = pe.matmul(dst[:, j:j + 1], ties[:, j, :], ones_bf[:, 0:1], start=False, stop=True)
                last.then_inc(rank_ready[b], 1)

            def period(at):
                if at.live(-1):
                    turn(at, 0)
                    turn(at, 1)
                if at.live(0):
                    scores(at)
                if at.live(1) and at.fixed >= 0:
                    queries(at)
                if at.live(-1):
                    turn(at, 2)
                if at.live(-2):
                    project(at)
                if at.live(-1):
                    values(at)
                if at.fixed in (AT_TURN, AT_RANK_ROW, AT_RANK):
                    pe.wait_ge(pt_lo_done, at.p * 3 - 1)
                if at.fixed == AT_TURN:
                    turn_scores(0, ps_t1)
                if at.fixed == AT_RANK_ROW:
                    rank_rows(0, ps_t1)
                if at.fixed == AT_RANK:
                    rank_cols(0, ps_t1)

            periods(pe, period)

            def gather(b):
                pe.wait_ge(sel_done[b], TILES)
                pe.wait_ge(x1_split[b], 1)
                pe.wait_ge(exp_done, 4 * UNITS)
                if b:
                    pe.wait_ge(xs_split[0], CH)
                for c in range(CH):
                    dst = ps_s3[:, c * KEEP:(c + 1) * KEEP]
                    for j in range(TILES):
                        t, cs = b * TILES + j, slice(c * P, (c + 1) * P)
                        pe.matmul(dst, x1_hi[:, t, cs], sel[:, t, :], start=(j == 0), stop=False)
                        last = pe.matmul(dst, x1_lo[:, t, cs], sel[:, t, :], start=False, stop=(j == TILES - 1))
                last.then_inc(gathered[b], 1)

            def hidden(b):
                pe.wait_ge(xs_split[b], CH)
                pe.wait_ge(y_lo_done, UNITS)
                pe.wait_ge(wf_split, len(WF_PERIODS))
                if b:
                    pe.wait_ge(gelu_done[0], FCH)
                for f in range(FCH):
                    if f == 6:
                        pe.wait_ge(gelu_done[b], 2)
                    for c in range(CH):
                        w = slice(c * FFN + f * P, c * FFN + (f + 1) * P)
                        last = product(hidden_bank(b, f), (wf_hi[:, w], wf_lo[:, w]),
                                       (xs_hi[:, b, c, :], xs_lo[:, b, c, :]), c == 0, c == CH - 1)
                    if f % 2:
                        last.then_inc(hid_ready[b], 1)

            def net_out(b):
                pe.wait_ge(out_taken, BATCH)
                for r in range(RCH):
                    if b:
                        pe.wait_ge(net_done[0], r + 1)
                    for f in range(FCH):
                        if r == 0:
                            pe.wait_ge(hid_split[b], f + 1)
                        w = slice(W2_AT + f * DIM, W2_AT + (f + 1) * DIM)
                        t = slice(r * P, (r + 1) * P)
                        last = product(net_bank(b, r), (hid_hi[:, b, f, t], hid_lo[:, b, f, t]),
                                       (wf_hi[:, w], wf_lo[:, w]), f == 0, f == FCH - 1)
                    last.then_inc(net_ready[b], 1)

            def scatter(b):
                pe.wait_ge(selT_done[b], RCH)
                pe.wait_ge(net_split[b], RCH)
                if b == 0:
                    pe.wait_ge(rank_done[1], 1)
                    pe.wait_ge(rank_row_done[1], 1)
                else:
                    pe.wait_ge(sum_done[0], TILES)
                for j in range(TILES):
                    dst = (ps_t0, ps_t1)[j // 2][:, (j % 2) * DIM:(j % 2 + 1) * DIM]
                    for q in range(RCH):
                        one = selT[:, b, q, j * P:(j + 1) * P]
                        pe.matmul(dst, one, net_hi[:, b, q, :], start=(q == 0), stop=False)
                        last = pe.matmul(dst, one, net_lo[:, b, q, :], start=False, stop=(q == RCH - 1))
                    if j % 2:
                        last.then_inc(scattered[b], 1)

            gather(0)
            hidden(0)
            net_out(0)
            turn_scores(1, ps_t0)
            rank_rows(1, ps_t1)
            pe.wait_ge(score_row_done[1], 1)
            rank_cols(1, ps_t0)
            gather(1)
            scatter(0)
            hidden(1)
            net_out(1)
            scatter(1)

        @block.scalar
        def _(act):
            def split_queries(k, head):
                wait(act, q_ready, k + 1)
                wait(act, scores_ready, k * 3)
                act.activation(qT_hi[:, :], ps_qy[:, :], ACT.Identity, bias=bias_cols[:, bass.ds(head, 1)],
                               scale=1.0).then_inc(q_hi_done, 1)

            for b in range(BATCH):
                for c in range(CH):
                    act.wait_ge(x_turned, CH * b + c + 1)
                    act.copy(xT_hi[b][:, c, :], (ps_t0, ps_t1)[c][:, :]).then_inc(x_hi_done, 1)
                act.wait_ge(kT_done, b + 1)
                act.mul(kT_hi[b][:, :], kT[b][:, :], SCALE).then_inc(kT_hi_done, 1)
                act.wait_ge(k_turned, b + 1)
                act.copy(k_hi[b][:, :, :], ps_t0[:, :].rearrange("p (j l) -> p j l", l=LAT)).then_inc(k_hi_done, 1)
                if b == 0:
                    act.wait_ge(bias_done, 1)
                    split_queries(0, 0)

            def exps(at, js):
                s = at.place(0)
                for j in js:
                    wait(act, negmax_done, at.p * 4 + (4 - j if j > 1 else 4))
                    act.activation(p_tile(s, j), score_bank[j], ACT.Exp, bias=negmax[:, s, j:j + 1],
                                   scale=1.0, accum_out=sums[:, s, j:j + 1]).then_inc(exp_done, 1)

            def turned(at, n):
                wait(act, pt_ready, at.p * 3 - 2 + n)
                dst = turns[n][2]
                act.copy(pT_hi[:, dst], turns[n][1][:, 0:dst.stop - dst.start]).then_inc(pt_hi_done, 1)

            def period(at):
                p = at.p
                if at.live(-2):
                    wait(act, y_ready, p - 1)
                    wait(act, proj_done, p - 2)
                    act.copy(yT_hi[:, :], ps_qy[:, :]).then_inc(y_hi_done, 1)
                if at.fixed - 1 == AT_TURN:
                    row_of_scores(0, ps_t1)
                if at.fixed - 1 == AT_RANK_ROW:
                    row_of_ranks(0, ps_t1)
                if at.fixed - 1 == AT_RANK:
                    col_of_ranks(0, ps_t1)
                if at.live(-1):
                    wait(act, y_ready, p - 1)
                    turned(at, 0)
                    turned(at, 1)
                if at.live(0):
                    wait(act, pt_ready, p * 3 - 3)
                    exps(at, (3, 2, 1, 0))
                if at.live(1) and at.fixed >= 0:
                    split_queries(p + 1, at.head(1))
                if at.live(-1):
                    turned(at, 2)
                if at.live(0):
                    wait(act, rinv_done, p + 1)
                    act.mul(p_tile(at.place(0), 3), p_tile(at.place(0), 3),
                            rinv[:, at.place(0), 3:4]).then_inc(norm_act, 1)
                if at.fixed == AT_TURN:
                    split_x1(0)

            def split_x1(b):
                act.wait_ge(ln_done[b], TILES)
                act.copy(x1_hi[:, b * TILES:(b + 1) * TILES, :], x1_of(b)).then_inc(x1_hi_done[b], 1)

            def row_of_scores(b, src):
                act.wait_ge(score_turned[b], 1)
                if b:
                    act.wait_ge(compared[0], 3 * TILES - 1)
                act.copy(score_row[:, :], src[:, :]).then_inc(score_row_done[b], 1)
                act.activation(e_neg[:, b, :], score[:, b, :], ACT.Exp, bias=0.0, scale=-1.0).then_inc(exp_neg[b], 1)

            def row_of_ranks(b, src):
                act.wait_ge(rank_row_ready[b], 1)
                if b:
                    act.wait_ge(selT_done[0], RCH)
                act.copy(rank_row[:, :], src[:, :]).then_inc(rank_row_done[b], 1)

            def col_of_ranks(b, src):
                act.wait_ge(rank_ready[b], 1)
                if b:
                    act.wait_ge(sel_done[0], TILES)
                act.copy(rank[:, :], src[:, 0:TILES]).then_inc(rank_done[b], 1)

            periods(act, period)

            def double_x1(b):
                act.wait_ge(x1_split[b], 1)
                act.wait_ge(dots_done[b], TILES)
                act.mul(x1_of(b), x1_of(b), 2.0).then_inc(x1_doubled[b], 1)

            def gelu(b, f):
                if f % 2 == 0:
                    act.wait_ge(hid_ready[b], f // 2 + 1)
                act.activation(hid[:, f, :], hidden_bank(b, f), ACT.Gelu_apprx_tanh,
                               bias=bias_cols[:, B_ONE + f:B_ONE + f + 1], scale=1.0).then_inc(gelu_done[b], 1)

            def chosen(b):
                act.wait_ge(gathered[b], 1)
                for c in range(CH):
                    act.copy(xs_hi[:, b, c, :], ps_s3[:, c * KEEP:(c + 1) * KEEP]).then_inc(xs_hi_done[b], 1)

            def net_high(b, r):
                act.wait_ge(net_done[b], r + 1)
                act.copy(net_hi[:, b, r, :], net[:, b, r, :]).then_inc(net_hi_done[b], 1)

            chosen(0)
            double_x1(0)
            for f in range(FCH):
                gelu(0, f)
                act.wait_ge(gelu_done[0], f + 1)
                act.copy(hid_hi[:, 0, f, :], hid[:, f, :]).then_inc(hid_hi_done[0], 1)
                if f == 3:
                    split_x1(1)
            row_of_scores(1, ps_t0)
            double_x1(1)
            for r in range(RCH):
                net_high(0, r)
            row_of_ranks(1, ps_t1)
            col_of_ranks(1, ps_t0)
            chosen(1)
            act.wait_ge(hid_split[0], FCH)
            for f in range(FCH):
                gelu(1, f)
            for r in range(RCH):
                net_high(1, r)

        @block.vector
        def _(dve):
            def queries_low(k, head):
                wait(dve, q_hi_done, k + 1)
                dve.scalar_tensor_tensor(qT_lo[:, :], ps_qy[:, :], bias_cols[:, bass.ds(head, 1)],
                                         qT_hi[:, :].bitcast(F32), ALU.add, ALU.subtract).then_inc(q_lo_done, 1)

            for b in range(BATCH):
                for c in range(CH):
                    dve.wait_ge(x_hi_done, CH * b + c + 1)
                    dve.tensor_tensor(xT_lo[b][:, c, :], (ps_t0, ps_t1)[c][:, :],
                                      xT_hi[b][:, c, :].bitcast(F32), ALU.subtract).then_inc(x_split, 1)
                if b == 0:
                    dve.wait_ge(bias_turned, 1)
                    dve.tensor_copy(bias_cols[:, :], ps_out[:, 0, 0:HEADS + 1 + FCH]).then_inc(bias_done, 1)
                    dve.wait_ge(bias_done, 1)
                dve.wait_ge(kT_ready, b + 1)
                dve.tensor_scalar(kT[b][:, :], ps_qy[:, :], bias_cols[:, B_LAT:B_LAT + 1], None,
                                  ALU.add).then_inc(kT_done, 1)
                dve.wait_ge(kT_hi_done, b + 1)
                dve.wait_ge(kT_done, b + 1)
                dve.scalar_tensor_tensor(kT_lo[b][:, :], kT[b][:, :], SCALE, kT_hi[b][:, :].bitcast(F32),
                                         ALU.mult, ALU.subtract).then_inc(kT_split, 1)
                dve.wait_ge(k_hi_done, b + 1)
                dve.tensor_tensor(k_lo[b][:, :, :], ps_t0[:, :].rearrange("p (j l) -> p j l", l=LAT),
                                  k_hi[b][:, :, :].bitcast(F32), ALU.subtract).then_inc(k_split, 1)
                if b == 0:
                    queries_low(0, 0)

            def start_x1(b):
                dve.wait_ge(rows_in, 64)
                dve.tensor_tensor(x1_of(b), x_nat[:, b * TILES:(b + 1) * TILES, :],
                                  bproj_all[:, :].unsqueeze(1).broadcast_to([P, TILES, DIM]),
                                  ALU.add).then_inc(x1_started, 1)

            def maxima(at, js):
                s = at.place(0)
                for j in js:
                    if j:
                        wait(dve, scores_ready, at.p * 3 + {3: 1, 2: 2, 1: 3}[j])
                    dve.tensor_reduce(negmax[:, s, j:j + 1], score_bank[j], AX_X, ALU.max,
                                      negate=True).then_inc(negmax_done, 1)

            def turned(at, n):
                wait(dve, pt_hi_done, at.p * 3 - 2 + n)
                dst = turns[n][2]
                dve.tensor_tensor(pT_lo[:, dst], turns[n][1][:, 0:dst.stop - dst.start],
                                  pT_hi[:, dst].bitcast(F32), ALU.subtract).then_inc(pt_lo_done, 1)

            def period(at):
                p = at.p
                if at.live(-2):
                    wait(dve, y_hi_done, p - 1)
                    dve.tensor_tensor(yT_lo[:, :], ps_qy[:, :], yT_hi[:, :].bitcast(F32),
                                      ALU.subtract).then_inc(y_lo_done, 1)
                if at.live(0):
                    maxima(at, (3, 2))
                if at.live(-1):
                    turned(at, 0)
                if at.live(0):
                    maxima(at, (1, 0))
                if at.live(-1):
                    turned(at, 1)
                if at.live(1) and at.fixed >= 0:
                    queries_low(p + 1, at.head(1))
                if at.live(-1):
                    turned(at, 2)
                if at.live(0):
                    s = at.place(0)
                    wait(dve, exp_done, p * 4 + 4)
                    dve.reciprocal(rinv[:, s, :], sums[:, s, :]).then_inc(rinv_done, 1)
                    wait(dve, rinv_done, p + 1)
                    for j in (2, 1, 0):
                        dve.tensor_scalar(p_tile(s, j), p_tile(s, j), rinv[:, s, j:j + 1], None,
                                          ALU.mult).then_inc(norm_dve, 1)
                if at.fixed in (0, 1):
                    start_x1(at.fixed)
                if at.live(-2) and at.fixed - 2 == at.batch(-2) * HEADS + HEADS - 1:
                    b = at.batch(-2)
                    dve.wait_ge(proj_done, (b + 1) * HEADS)
                    dve.wait_ge(x1_started, b + 1)
                    dve.tensor_tensor(x1_of(b), ps_out[:, :, :], x1_of(b), ALU.add).then_inc(out_taken, 1)
                if at.fixed == AT_STATS:
                    layernorm_stats(0, 0)
                if at.fixed == AT_APPLY:
                    layernorm_apply(0, 0)
                    router_scores(0)
                if at.fixed == AT_COMPARE:
                    compare(0)
                if at.fixed == AT_SELECT:
                    select(0)

            def layernorm_stats(b, which):
                k, n = which * BATCH + b, which * TILES
                dve.wait_ge(*((out_taken, b + 1) if which == 0 else (sum_done[b], TILES)))
                for j in range(TILES):
                    dve.bn_stats(st[:, k, j, :], x1[:, b * TILES + j, :]).then_inc(stats_done[b], 1)
                for j in range(TILES):
                    dve.wait_ge(stats_done[b], n + j + 1)
                    dve.bn_aggr(mv[:, k, j, :], st[:, k, j, :]).then_inc(aggr_done[b], 1)
                dve.wait_ge(aggr_done[b], n + TILES)
                dve.tensor_scalar(ve[:, k, :], mv[:, k, :, 1], EPS, None, ALU.add).then_inc(var_done[b], 1)

            def layernorm_apply(b, which):
                k = which * BATCH + b
                dve.wait_ge(rstd_done[b], which + 1)
                for j in range(TILES):
                    r = x1[:, b * TILES + j, :]
                    dve.tensor_scalar(r, r, mv[:, k, j, 0:1], rstd[:, k, j:j + 1],
                                      ALU.subtract, ALU.mult).then_inc(ln_done[b], 1)

            def router_scores(b):
                if b == 0:
                    dve.wait_ge(consts, CONSTS)
                for j in range(TILES):
                    dve.wait_ge(ln_done[b], j + 1)
                    dve.scalar_tensor_tensor(sel[:, b * TILES + j, :], x1[:, b * TILES + j, :], 1.0,
                                             rw_all[:, :], ALU.mult, ALU.mult,
                                             accum_out=dots[:, b, j:j + 1]).then_inc(dots_done[b], 1)
                dve.wait_ge(dots_done[b], TILES)
                dve.tensor_scalar(score[:, b, :], dots[:, b, :], rb_all[:, 0:1], None, ALU.add).then_inc(score_done[b], 1)

            def compare(b):
                dve.wait_ge(score_row_done[b], 1)
                if b:
                    dve.wait_ge(rank_ready[0], 1)
                for t in range(TILES):
                    mine, own = score[:, b, t:t + 1], (t + 1) * P
                    dve.tensor_scalar(beats[:, t, 0:own], score_row[:, 0:own], mine, None,
                                      ALU.is_lt).then_inc(compared[b], 1)
                    if own < SEQ:
                        dve.tensor_scalar(beats[:, t, own:], score_row[:, own:], mine, None,
                                          ALU.is_le).then_inc(compared[b], 1)
                    dve.scalar_tensor_tensor(ties[:, t, :], score_row[:, t * P:own], mine, earlier[:, :],
                                             ALU.is_equal, ALU.mult).then_inc(compared[b], 1)

            def select(b):
                dve.wait_ge(rank_done[b], 1)
                for j in range(TILES):
                    dve.tensor_scalar(sel[:, b * TILES + j, :], iota_row[:, :], rank[:, j:j + 1], None,
                                      ALU.is_equal).then_inc(sel_done[b], 1)
                dve.wait_ge(rank_row_done[b], 1)
                for q in range(RCH):
                    dve.tensor_scalar(selT[:, b, q, :], rank_row[:, :], iota_col[:, q:q + 1], None,
                                      ALU.is_equal).then_inc(selT_done[b], 1)
                dve.wait_ge(exp_neg[b], 1)
                dve.tensor_scalar(e_one[:, b, :], e_neg[:, b, :], 1.0, None, ALU.add).then_inc(weight_half[b], 1)
                dve.wait_ge(weight_half[b], 1)
                dve.reciprocal(weight[:, b, :], e_one[:, b, :]).then_inc(weight_done[b], 1)

            periods(dve, period)

            def chosen_low(b):
                for c in range(CH):
                    dve.wait_ge(xs_hi_done[b], CH)
                    dve.tensor_tensor(xs_lo[:, b, c, :], ps_s3[:, c * KEEP:(c + 1) * KEEP],
                                      xs_hi[:, b, c, :].bitcast(F32), ALU.subtract).then_inc(xs_split[b], 1)

            def net_take(b, r):
                dve.wait_ge(net_ready[b], r + 1)
                dve.tensor_tensor(net[:, b, r, :], net_bank(b, r), b2_all[:, :], ALU.add).then_inc(net_done[b], 1)

            def net_low(b, r):
                dve.wait_ge(net_hi_done[b], r + 1)
                dve.tensor_tensor(net_lo[:, b, r, :], net[:, b, r, :], net_hi[:, b, r, :].bitcast(F32),
                                  ALU.subtract).then_inc(net_split[b], 1)

            def add_up(b):
                dve.wait_ge(weight_done[b], 1)
                dve.wait_ge(x1_doubled[b], 1)
                for j in range(TILES):
                    r = x1[:, b * TILES + j, :]
                    dve.wait_ge(scattered[b], j // 2 + 1)
                    dve.scalar_tensor_tensor(r, (ps_t0, ps_t1)[j // 2][:, (j % 2) * DIM:(j % 2 + 1) * DIM],
                                             weight[:, b, j:j + 1], r, ALU.mult, ALU.add).then_inc(sum_done[b], 1)

            chosen_low(0)
            layernorm_stats(1, 0)
            layernorm_apply(1, 0)
            router_scores(1)
            compare(1)
            for r in range(RCH):
                net_take(0, r)
            select(1)
            for r in range(RCH):
                net_low(0, r)
            chosen_low(1)
            add_up(0)
            for f in range(FCH):
                dve.wait_ge(gelu_done[1], f + 1)
                dve.tensor_copy(hid_hi[:, 1, f, :], hid[:, f, :]).then_inc(hid_hi_done[1], 1)
                dve.wait_ge(hid_hi_done[1], f + 1)
                dve.tensor_tensor(hid_lo[:, 1, f, :], hid[:, f, :], hid_hi[:, 1, f, :].bitcast(F32),
                                  ALU.subtract).then_inc(hid_split[1], 1)
            layernorm_stats(0, 1)
            layernorm_apply(0, 1)
            for r in range(RCH):
                net_take(1, r)
                net_low(1, r)
            add_up(1)
            layernorm_stats(1, 1)
            layernorm_apply(1, 1)

        @block.gpsimd
        def _(pool):
            def split(hi, lo, src, hi_done, split_done, number):
                pool.tensor_tensor(hi, src, zero[:, 0:src.free_size()].rearrange("p (a c) -> p a c", a=src.shape[1]) if len(src.shape) == 3 else
                                   zero[:, 0:src.free_size()], ALU.add).then_inc(hi_done, 1)
                wait(pool, hi_done, number + 1)
                pool.tensor_tensor(lo, src, hi.bitcast(F32), ALU.subtract).then_inc(split_done, 1)

            def split_wd(unit, place, use):
                wait(pool, wd_in[place], (use + 1) * 16)
                wait(pool, q_ready, unit - 1)
                split(wd_hi[place][:], wd_lo[place][:], wd_raw[place][:], wd_hi_done, wd_split, unit)

            pool.memset(ident[:, :], 0.0).then_inc(filled, 1)
            pool.memset(zero[:, :], 0.0).then_inc(filled, 1)
            pool.wait_ge(filled, 2)
            pool.affine_select(out=ident[:, :], in_=ident[:, :], compare_op=ALU.not_equal, fill=1.0, base=0,
                               pattern=[[-1, P]], channel_multiplier=1).then_inc(ident_done, 1)
            pool.wait_ge(wlat_in, 16)
            split(wlat_hi[:], wlat_lo[:], wlat_raw[:], wlat_hi_done, wlat_split, 0)
            split_wd(0, 0, 0)
            pool.memset(mask_bf[:, :], 0.0).then_inc(filled, 1)
            pool.memset(earlier[:, :], 1.0).then_inc(filled, 1)
            pool.wait_ge(filled, 4)
            pool.affine_select(out=mask_bf[:, :], in_=mask_bf[:, :], compare_op=ALU.is_ge, fill=MASKED, base=0,
                               pattern=[[-1, P]], channel_multiplier=1).then_inc(consts, 1)
            pool.wait_ge(ident_done, 1)
            pool.tensor_copy(ident_bf[:, :], ident[:, :]).then_inc(consts, 1)
            pool.memset(pT_hi[:, 0:P].bitcast(F32), 0.0).then_inc(consts, 1)
            pool.memset(pT_lo[:, 0:P].bitcast(F32), 0.0).then_inc(consts, 1)
            pool.affine_select(out=earlier[:, :], in_=earlier[:, :], compare_op=ALU.is_gt, fill=0.0,
                               base=0, pattern=[[1, P]], channel_multiplier=-1).then_inc(consts, 1)

            def period(at):
                if at.live(2):
                    split_wd(at.p + 2, at.place(2), at.use(2))
                if at.live(-1):
                    s = at.place(-1)
                    wait(pool, wp_in[s], (at.use(-1) + 1) * 16)
                    wait(pool, proj_done, at.p - 2)
                    split(wp_hi[s][:], wp_lo[s][:], wp_raw[s][:], wp_hi_done, wp_split, at.p - 1)
                if at.fixed == 1:
                    pool.memset(ones_bf[:, :], 1.0).then_inc(consts, 1)
                    pool.iota(iota_row[:, :], pattern=[[1, KEEP]], base=0, channel_multiplier=0,
                              allow_small_or_imprecise_dtypes=True).then_inc(consts, 1)
                    pool.iota(iota_col[:, :], pattern=[[P, RCH]], base=0, channel_multiplier=1,
                              allow_small_or_imprecise_dtypes=True).then_inc(consts, 1)
                    pool.memset(minus_half[:, :], -0.5).then_inc(consts, 1)
                if at.fixed in WF_PERIODS:
                    n = WF_PERIODS.index(at.fixed)
                    if n == 0:
                        pool.wait_ge(w1_in, 16)
                        pool.wait_ge(w2_in, 16)
                    part = slice(n * WF_PART, (n + 1) * WF_PART)
                    split(wf_hi[:, part], wf_lo[:, part], wf_raw[:, part], wf_hi_done, wf_split, n)
                if at.fixed == AT_STATS:
                    inverse_deviation(0, 0)
                if at.fixed == AT_TURN:
                    x1_low(0)

            def inverse_deviation(b, which):
                k = which * BATCH + b
                pool.wait_ge(consts, CONSTS)
                pool.wait_ge(var_done[b], which + 1)
                pool.tensor_tensor(rstd[:, k, :], ve[:, k, :], minus_half[:, :], ALU.pow).then_inc(rstd_done[b], 1)

            def x1_low(b):
                pool.wait_ge(x1_hi_done[b], 1)
                pool.tensor_tensor(x1_lo[:, b * TILES:(b + 1) * TILES, :], x1_of(b),
                                   x1_hi[:, b * TILES:(b + 1) * TILES, :].bitcast(F32), ALU.subtract).then_inc(x1_split[b], 1)

            periods(pool, period)
            inverse_deviation(1, 0)
            for f in range(FCH):
                pool.wait_ge(hid_hi_done[0], f + 1)
                pool.tensor_tensor(hid_lo[:, 0, f, :], hid[:, f, :], hid_hi[:, 0, f, :].bitcast(F32),
                                   ALU.subtract).then_inc(hid_split[0], 1)
                if f == 3:
                    x1_low(1)
            inverse_deviation(0, 1)
            inverse_deviation(1, 1)
    return nc


_INS = ["L0_attn_x", "L0_attn_W_lat", "L0_attn_b_lat", "L0_attn_W_d", "L0_attn_b_d", "L0_attn_W_proj",
        "L0_attn_b_proj", "L0_ffn_router_weight", "L0_ffn_router_bias", "L0_ffn_w1", "L0_ffn_b1",
        "L0_ffn_w2", "L0_ffn_b2"]


def kernel(**inputs):
    import numpy as np
    from concourse import bacc
    from concourse.bass_utils import run_bass_kernel_spmd

    nc = bacc.Bacc("TRN2", target_bir_lowering=False, num_devices=1)
    arrays, args = {}, []
    for name in _INS:
        a = np.ascontiguousarray(inputs[name])
        arrays[f"in_{name}"] = a
        args.append(nc.dram_tensor(f"in_{name}", a.shape, mybir.dt.from_np(a.dtype), kind="ExternalInput").ap())
    out = nc.dram_tensor("out", (BATCH, SEQ, DIM), F32, kind="ExternalOutput").ap()
    mk_layer_kernel(nc, *args, out)
    r = run_bass_kernel_spmd(nc, [arrays], core_ids=[0])
    return r.results[0]["out"]
```

```python
import math
from contextlib import ExitStack

import concourse.bass as bass
from concourse import mybir

F32 = mybir.dt.float32
F32R = mybir.dt.float32r
BF16 = mybir.dt.bfloat16
ACT = mybir.ActivationFunctionType
ALU = mybir.AluOpType

P = 128
BATCH, SEQ, DIM = 2, 512, 256
HEADS, LAT = 16, 128
FFN = 1024
KEEP = SEQ // 2
TILES = SEQ // P
CH = DIM // P
FCH = FFN // P
RCH = KEEP // P
UNITS = BATCH * HEADS
SCALE = 1.0 / math.sqrt(LAT)
EPS = 1e-5
MASKED = -1.0e38

P_OFF = [P * (j * (j + 1) // 2) for j in range(TILES)]
P_COLS = P * TILES * (TILES + 1) // 2
PT_OFF = {2: 0, 1: 2 * P, 0: 5 * P}
PT_COLS = 9 * P


def mk_layer_kernel(nc, x, W_lat, b_lat, W_d, b_d, W_proj, b_proj, router_w, router_b,
                    w1, b1, w2, b2, out):
    with ExitStack() as top:
        def sb(name, shape, dt=F32, stack=top):
            return stack.enter_context(nc.sbuf_tensor(name, shape, dt))

        def sem(name):
            return top.enter_context(nc.semaphore(name))

        x1 = sb("x1", [P, BATCH * TILES, DIM])
        W2_AT = CH * FFN
        WF_COLS = W2_AT + FCH * DIM
        wf_raw = sb("wf_raw", [P, WF_COLS])
        wf_hi, wf_lo = (sb(n, [P, WF_COLS], F32R) for n in ("wf_hi", "wf_lo"))
        still = sb("still", [P, SEQ], BF16)
        ident = sb("ident", [P, P])
        ones_bf = sb("ones_bf", [P, 1], BF16)
        mask_row = sb("mask_row", [P, SEQ])
        earlier = sb("earlier", [P, P], BF16)
        iota_row = sb("iota_row", [P, KEEP])
        iota_col = sb("iota_col", [P, RCH])
        B_LAT, B_ONE, BIASES = HEADS, HEADS + 1, HEADS + 1 + FCH
        bias_rows = sb("bias_rows", [BIASES, P])
        bias_cols = sb("bias_cols", [P, BIASES])
        bproj_all = sb("bproj_all", [P, DIM])
        b2_all = sb("b2_all", [P, DIM])
        rw_all = sb("rw_all", [P, DIM])
        rb_all = sb("rb_all", [P, 1])
        zero = sb("zero", [P, 512])
        minus_half = sb("minus_half", [P, TILES])
        negmax = sb("negmax", [P, 2, TILES])
        sums = sb("sums", [P, 2, TILES])
        rinv = sb("rinv", [P, 2, TILES])
        st = sb("st", [P, BATCH * 2, TILES, 6])
        mv = sb("mv", [P, BATCH * 2, TILES, 2])
        ve = sb("ve", [P, BATCH * 2, TILES])
        rstd = sb("rstd", [P, BATCH * 2, TILES])
        z_sum, minus_mean, squares = (sb(n, [P, TILES]) for n in ("z_sum", "minus_mean", "squares"))
        squared = sb("squared", [P, TILES, DIM])
        dots = sb("dots", [P, BATCH, TILES])
        score = sb("score", [P, BATCH, TILES])
        score_row = sb("score_row", [P, SEQ])
        beats = sb("beats", [P, TILES, SEQ], BF16)
        ties = sb("ties", [P, TILES, P], BF16)
        rank_row = sb("rank_row", [P, SEQ])
        rank = sb("rank", [P, TILES])
        half_tanh = sb("half_tanh", [P, BATCH, TILES])
        ones_row = sb("ones_row", [1, P], F32R)
        b2_hi, b2_lo = sb("b2_hi", [1, DIM], F32R), sb("b2_lo", [1, DIM], F32R)
        weight = sb("weight", [P, BATCH, TILES])
        x1_hi = sb("x1_hi", [P, BATCH * TILES, DIM], F32R)
        x1_lo = sb("x1_lo", [P, BATCH * TILES, DIM], F32R)
        sel = sb("sel", [P, BATCH * TILES, KEEP], F32R)
        selT = sb("selT", [P, BATCH, RCH, SEQ], F32R)

        bank = [top.enter_context(nc.psum_tensor(f"bank{i}", [P, 512], F32)) for i in range(6)]
        ps_s3, ps_s2, ps_s10, ps_t0, ps_t1, ps_y = bank
        ps_q = ps_s3
        ps_out = top.enter_context(nc.psum_tensor("ps_out", [P, TILES, DIM], F32))

        def sems(name):
            return [sem(f"{name}{b}") for b in range(BATCH)]

        x_in = [[sem(f"x_in{b}_{half}") for half in range(2)] for b in range(BATCH)]
        wd_in, wp_in = sems("wd_in"), sems("wp_in")
        wlat_in, bias_in, rows_in, w1_in, w2_in = (sem(n) for n in ("wlat_in", "bias_in", "rows_in", "w1_in", "w2_in"))
        still_filled, filled, ident_done, consts = (
            sem(n) for n in ("still_filled", "filled", "ident_done", "consts"))
        b2_hi_done, b2_split = sem("b2_hi_done"), sem("b2_split")
        bias_turned, bias_done = sem("bias_turned"), sem("bias_done")
        wlat_hi_done, wlat_split = sem("wlat_hi_done"), sem("wlat_split")
        x_turned, x_hi_done, x_split, x1_started = sem("x_turned"), sem("x_hi_done"), sem("x_split"), sem("x1_started")
        kT_ready, kT_done, kT_hi_done, kT_split = (
            sem(n) for n in ("kT_ready", "kT_done", "kT_hi_done", "kT_split"))
        k_turned, k_last_done, k_hi_done, k_split = (
            sem(n) for n in ("k_turned", "k_last_done", "k_hi_done", "k_split"))
        wd_hi_done, wd_split = sem("wd_hi_done"), sem("wd_split")
        wp_hi_done, wp_split = sem("wp_hi_done"), sem("wp_split")
        wf_hi_done, wf_split = sem("wf_hi_done"), sem("wf_split")
        q_ready, q_first_done, q_hi_done, q_lo_done = (
            sem(n) for n in ("q_ready", "q_first_done", "q_hi_done", "q_lo_done"))
        mask_done = sem("mask_done")
        scores_ready, negmax_done, exp_done, rinv_done = (
            sem(n) for n in ("scores_ready", "negmax_done", "exp_done", "rinv_done"))
        norm_act, norm_dve = sem("norm_act"), sem("norm_dve")
        pt_ready, pt_last_done, pt_hi_done, pt_lo_done = (
            sem(n) for n in ("pt_ready", "pt_last_done", "pt_hi_done", "pt_lo_done"))
        y_ready, y_hi_done, y_lo_done = sem("y_ready"), sem("y_hi_done"), sem("y_lo_done")
        proj_done, proj_half, out_taken = sem("proj_done"), sem("proj_half"), sem("out_taken")
        stats_done, aggr_done, var_done, rstd_done, ln_done = (
            sems(n) for n in ("stats_done", "aggr_done", "var_done", "rstd_done", "ln_done"))
        dots_done, score_done, score_turned, score_row_done = (
            sems(n) for n in ("dots_done", "score_done", "score_turned", "score_row_done"))
        compared, rank_row_ready, rank_ready, rank_row_done, rank_done = (
            sems(n) for n in ("compared", "rank_row_ready", "rank_ready", "rank_row_done", "rank_done"))
        sel_done, selT_done, tanh_done, weight_done = (
            sems(n) for n in ("sel_done", "selT_done", "tanh_done", "weight_done"))
        x1_hi_done, x1_split, x1_doubled = sems("x1_hi_done"), sems("x1_split"), sems("x1_doubled")
        gathered, xs_hi_done, xs_split = sems("gathered"), sems("xs_hi_done"), sems("xs_split")
        hid_ready, gelu_done, hid_hi_done, hid_split = (
            sems(n) for n in ("hid_ready", "gelu_done", "hid_hi_done", "hid_split"))
        net_ready, net_hi_done, net_split = (
            sems(n) for n in ("net_ready", "net_hi_done", "net_split"))
        minus_mean_done, squares_done = sem("minus_mean_done"), sem("squares_done")
        scattered, sum_done, stored = sems("scattered"), sems("sum_done"), sems("stored")

        def wait(eng, s, value):
            if not isinstance(value, int) or value > 0:
                eng.wait_ge(s, value)

        att = ExitStack()
        x_nat = sb("x_nat", [P, BATCH * TILES, DIM], F32, att)
        wlat_raw = sb("wlat_raw", [P, CH, LAT], F32, att)
        wlat_hi, wlat_lo = sb("wlat_hi", [P, CH, LAT], F32R, att), sb("wlat_lo", [P, CH, LAT], F32R, att)
        xT_hi = [sb(f"xT_hi{b}", [P, CH, SEQ], F32R, att) for b in range(BATCH)]
        xT_lo = [sb(f"xT_lo{b}", [P, CH, SEQ], F32R, att) for b in range(BATCH)]
        kT = [sb(f"kT{b}", [P, SEQ], F32, att) for b in range(BATCH)]
        kT_hi = [sb(f"kT_hi{b}", [P, SEQ], F32R, att) for b in range(BATCH)]
        kT_lo = [sb(f"kT_lo{b}", [P, SEQ], F32R, att) for b in range(BATCH)]
        k_hi = [sb(f"k_hi{b}", [P, TILES - 1, LAT], F32R, att) for b in range(BATCH)]
        k_lo = [sb(f"k_lo{b}", [P, TILES - 1, LAT], F32R, att) for b in range(BATCH)]
        k_last = [sb(f"k_last{b}", [P, LAT], F32, att) for b in range(BATCH)]
        wd_raw = [sb(f"wd_raw{s}", [P, CH, LAT], F32, att) for s in range(2)]
        wd_hi = [sb(f"wd_hi{s}", [P, CH, LAT], F32R, att) for s in range(2)]
        wd_lo = [sb(f"wd_lo{s}", [P, CH, LAT], F32R, att) for s in range(2)]
        wp_raw = [sb(f"wp_raw{s}", [P, DIM], F32, att) for s in range(2)]
        wp_hi = [sb(f"wp_hi{s}", [P, DIM], F32R, att) for s in range(2)]
        wp_lo = [sb(f"wp_lo{s}", [P, DIM], F32R, att) for s in range(2)]
        qT_first = [sb(f"qT_first{s}", [P, P], F32, att) for s in range(2)]
        qT_hi = [sb(f"qT_hi{s}", [P, SEQ], F32R, att) for s in range(2)]
        qT_lo = [sb(f"qT_lo{s}", [P, SEQ], F32R, att) for s in range(2)]
        yT_hi, yT_lo = sb("yT_hi", [P, SEQ], F32R, att), sb("yT_lo", [P, SEQ], F32R, att)
        probs = [sb(f"probs{s}", [P, P_COLS], F32, att) for s in range(2)]
        pT_last = sb("pT_last", [P, P], F32, att)
        pT_hi, pT_lo = sb("pT_hi", [P, PT_COLS], F32R, att), sb("pT_lo", [P, PT_COLS], F32R, att)
        att.close()
        xs_hi = sb("xs_hi", [P, BATCH, CH, KEEP], F32R)
        xs_lo = sb("xs_lo", [P, BATCH, CH, KEEP], F32R)
        hid = sb("hid", [P, FCH, KEEP])
        gelu_first = sb("gelu_first", [P, 1])
        hid_hi = sb("hid_hi", [P, BATCH, FCH, KEEP], F32R)
        hid_lo = sb("hid_lo", [P, BATCH, FCH, KEEP], F32R)
        net_hi = sb("net_hi", [P, BATCH, RCH, DIM], F32R)
        net_lo = sb("net_lo", [P, BATCH, RCH, DIM], F32R)

        def p_tile(s, j):
            return probs[s][:, P_OFF[j]:P_OFF[j] + (j + 1) * P]

        score_bank = {3: ps_s3[:, :], 2: ps_s2[:, 0:3 * P], 1: ps_s10[:, 2 * P:4 * P], 0: ps_s10[:, 0:P]}

        turns = [([0], ps_t0, ps_t0[:, :], slice(PT_OFF[0], PT_OFF[0] + 4 * P)),
                 ([1], ps_t1, ps_t1[:, 0:3 * P], slice(PT_OFF[1], PT_OFF[1] + 3 * P)),
                 ([3, 2], ps_t0, ps_t0[:, P:3 * P], slice(PT_OFF[2], PT_OFF[2] + 2 * P))]

        class Period:

            def __init__(self, p, fixed, turn):
                self.p, self.fixed, self.turn = p, fixed, turn

            def live(self, k):
                return 0 <= self.fixed + k < UNITS

            def batch(self, k):
                return (self.fixed + k) // HEADS

            def place(self, k):
                return (self.fixed + k) % 2

            def use(self, k):
                return self.turn + (self.fixed + k) // 2

            def head(self, k):
                return self.p + (k - self.batch(k) * HEADS)

        LOOPS = [(3, 5)]
        LAST = UNITS + 2

        def periods(eng, body):
            p = -1
            for first, times in LOOPS + [(LAST, 0)]:
                for q in range(p, first):
                    body(Period(q, q, 0))
                if times:
                    with eng.Fori(0, times) as i:
                        for q in range(first, first + 2):
                            body(Period(i * 2 + q, q, i))
                p = first + 2 * times

        WAKING, AWAKE = 6, 3
        CONSTS = 6
        AT_OUT = HEADS + 1
        (AT_STATS, AT_VARIANCE, AT_APPLY, AT_SCORE, AT_TURN, AT_COMPARE, AT_COMPARE_2, AT_RANK,
         AT_SELECT, AT_SELECT_T) = range(AT_OUT + 1, AT_OUT + 11)
        WF_PERIODS = range(13, 29)
        WF_PART = WF_COLS // len(WF_PERIODS)

        def x1_of(b):
            return x1[:, b * TILES:(b + 1) * TILES, :]

        hidden_banks = [ps_s10, ps_s3, ps_s2, ps_y]

        def hidden_bank(f):
            return hidden_banks[f % len(hidden_banks)][:, 0:KEEP]

        def net_bank(b, r):
            return ps_out[:, 2 * r + b, :]

        def scatter_bank(b, j):
            if b:
                return (ps_t0, ps_t1, ps_s2, ps_s3)[j][:, 0:DIM]
            return (ps_t0, ps_t1)[j // 2][:, (j % 2) * DIM:(j % 2 + 1) * DIM]

        def chosen_bank(c):
            return (ps_s3, ps_s2)[c][:, 0:KEEP]

        ps_kT = ps_out[:, 0:2, :].rearrange("p a d -> p (a d)")
        ps_k = ps_out[:, 2:4, :].rearrange("p a d -> p (a d)")

        block = top.enter_context(nc.Block())

        @block.sync
        def _(sp):
            wd = W_d.rearrange("(c p) n -> p c n", p=P)

            def load_wd(unit, place, head):
                wait(sp, wd_split, unit - 1)
                sp.dma_start(wd_raw[place][:], wd[:, :, bass.ds(head * LAT, LAT)]).then_inc(wd_in[place], 16)

            def load_wp(unit, place, head):
                wait(sp, wp_split, unit - 1)
                sp.dma_start(wp_raw[place][:], W_proj[bass.ds(head * LAT, LAT), :]).then_inc(wp_in[place], 16)

            def load_x(b):
                for j in range(0, TILES, 2):
                    sp.dma_start(x_nat[:, b * TILES + j:b * TILES + j + 2, :],
                                 x[b, j * P:(j + 2) * P].rearrange("(j p) d -> p j d", p=P)).then_inc(x_in[b][j // 2], 16)

            load_x(0)
            sp.dma_start(wlat_raw[:], W_lat.rearrange("(c p) l -> p c l", p=P)).then_inc(wlat_in, 16)
            load_wd(0, 0, 0)
            sp.dma_start(bias_rows[0:HEADS, :], b_d.rearrange("(h l) -> h l", l=LAT)).then_inc(bias_in, 16)
            sp.dma_start(bias_rows[B_LAT:B_LAT + 1, :], b_lat.rearrange("(a l) -> a l", a=1)).then_inc(bias_in, 16)
            sp.dma_start(bias_rows[B_ONE:B_ONE + FCH, :], b1.rearrange("(f l) -> f l", l=P)).then_inc(bias_in, 16)
            load_wd(1, 1, 1)
            load_x(1)
            load_wp(0, 0, 0)
            for dst, src in ((bproj_all, b_proj), (b2_all, b2), (rw_all, router_w), (rb_all, router_b)):
                n = src.shape[0]
                sp.dma_start(dst[:], src.rearrange("(a n) -> a n", a=1).broadcast_to([P, n])).then_inc(rows_in, 16)

            def period(at):
                if at.live(3) and at.fixed >= -1:
                    load_wd(at.p + 3, at.place(3), at.head(3))
                if at.live(0) and at.fixed >= 1:
                    load_wp(at.p, at.place(0), at.head(0))
                if at.fixed == 1:
                    sp.dma_start(wf_raw[:, 0:W2_AT].rearrange("p (c f) -> p c f", c=CH),
                                 w1.rearrange("(c p) f -> p c f", p=P)).then_inc(w1_in, 16)
                    sp.dma_start(wf_raw[:, W2_AT:].rearrange("p (f d) -> p f d", f=FCH),
                                 w2.rearrange("(f p) d -> p f d", p=P)).then_inc(w2_in, 16)

            periods(sp, period)
            STORES = [(0, 0, 2), (0, 2, 4), (1, 0, 2), (1, 2, 3), (1, 3, 4)]
            for b, j0, j1 in STORES:
                sp.wait_ge(ln_done[b], TILES + j1)
                sp.dma_start(out[b, j0 * P:j1 * P].rearrange("(j p) d -> p j d", p=P),
                             x1[:, b * TILES + j0:b * TILES + j1, :]).then_inc(stored[b], 16)
            for b in range(BATCH):
                sp.wait_ge(stored[b], 16 * len([st for st in STORES if st[0] == b]))

        @block.tensor
        def _(pe):
            def product(dst, left, right, first=True, last=True, check=False):
                (lh, ll), (rh, rl) = left, right
                pe.matmul(dst, lh, rh, start=first, stop=False, skip_group_check=check)
                pe.matmul(dst, lh, rl, start=False, stop=False, skip_group_check=check)
                return pe.matmul(dst, ll, rh, start=False, stop=last, skip_group_check=check)

            def turn_x(b):
                for half in range(2):
                    pe.wait_ge(x_in[b][half], 16)
                    for c in range(CH):
                        dst = (ps_t0, ps_t1)[c]
                        if b and half == 0:
                            pe.wait_ge(x_split, c + 1)
                        for j in range(2 * half, 2 * half + 2):
                            last = pe.transpose(dst[:, j * P:(j + 1) * P],
                                                x_nat[:, b * TILES + j, c * P:(c + 1) * P], ident[:, :])
                        if half:
                            last.then_inc(x_turned, 1)

            def project_k(b):
                pe.wait_ge(wlat_split, 1)
                if b:
                    pe.wait_ge(kT_done, b)
                    pe.wait_ge(kT_split, b)
                for c in range(CH):
                    pe.wait_ge(x_split, CH * b + c + 1)
                    last = product(ps_kT, (wlat_hi[:, c, :], wlat_lo[:, c, :]),
                                   (xT_hi[b][:, c, :], xT_lo[b][:, c, :]), c == 0, c == CH - 1)
                last.then_inc(kT_ready, 1)

            def turn_k(b):
                pe.wait_ge(kT_done, b + 1)
                if b:
                    pe.wait_ge(k_split, b)
                for j in range(TILES):
                    last = pe.transpose(ps_k[:, j * P:(j + 1) * P], kT[b][:, j * P:(j + 1) * P], ident[:, :])
                last.then_inc(k_turned, 1)

            def keep_awake(times):
                for _ in range(times):
                    pe.matmul(ps_s3[:, :], still[:, 0:P], still[:, :], start=True, stop=True)

            pe.wait_ge(still_filled, 1)
            keep_awake(WAKING)

            pe.wait_ge(ident_done, 1)
            turn_x(0)
            pe.wait_ge(bias_in, 48)
            pe.transpose(ps_s2[:, 0:BIASES], bias_rows[:, :], ident[0:BIASES, 0:BIASES]).then_inc(bias_turned, 1)
            keep_awake(AWAKE)
            project_k(0)
            pe.wait_ge(wd_split, 1)
            for c in range(CH):
                last = product(ps_q[:, :], (wd_hi[0][:, c, :], wd_lo[0][:, c, :]),
                               (xT_hi[0][:, c, :], xT_lo[0][:, c, :]), c == 0, c == CH - 1)
            last.then_inc(q_ready, 1)
            turn_x(1)
            turn_k(0)
            pe.wait_ge(bias_done, 1)

            def scores(at, js):
                p, b, s = at.p, at.batch(0), at.place(0)
                if at.fixed == b * HEADS:
                    pe.wait_ge(kT_split, b + 1)
                    pe.wait_ge(kT_done, b + 1)
                for j in js:
                    n = (j + 1) * P
                    dst = score_bank[j]
                    if j == 3:
                        wait(pe, q_lo_done, p + 1)
                    if j:
                        wait(pe, negmax_done, p * 4 - {3: 3, 2: 2, 1: 0}[j])
                    t = slice(j * P, (j + 1) * P)
                    if j:
                        last = product(dst, (qT_hi[s][:, t], qT_lo[s][:, t]), (kT_hi[b][:, 0:n], kT_lo[b][:, 0:n]))
                    else:
                        wait(pe, q_first_done, p + 1)
                        last = pe.matmul(dst, qT_first[s][:, :], kT[b][:, 0:P], start=True, stop=True)
                    if j != 1:
                        last.then_inc(scores_ready, 1)

            def turn(at, n):
                p, s = at.p, at.place(-1)
                tiles, dst, _, _ = turns[n]
                if n == 0:
                    wait(pe, norm_act, p)
                    wait(pe, norm_dve, p * 3)
                wait(pe, pt_lo_done, p * 3 - (3, 4, 2)[n])
                if n == 1 and at.fixed - 1 in (AT_TURN, AT_SELECT, AT_RANK):
                    pe.wait_ge({AT_TURN: score_row_done, AT_SELECT: rank_row_done, AT_RANK: rank_done}[at.fixed - 1][0], 1)
                if at.fixed == 1 and n < CH:
                    pe.wait_ge(x_split, CH + n + 1)
                a = 0
                for i in tiles:
                    for j in range(i, TILES):
                        last = pe.transpose(dst[:, a:a + P], p_tile(s, j)[:, i * P:(i + 1) * P], ident[:, :])
                        a += P
                last.then_inc(pt_ready, 1)

            def queries(at):
                b, s = at.batch(1), at.place(1)
                wait(pe, wd_split, at.p + 2)
                wait(pe, negmax_done, at.p * 4 + 1)
                for c in range(CH):
                    last = product(ps_q[:, :], (wd_hi[s][:, c, :], wd_lo[s][:, c, :]),
                                   (xT_hi[b][:, c, :], xT_lo[b][:, c, :]), c == 0, c == CH - 1)
                last.then_inc(q_ready, 1)

            def project(at):
                b, s = at.batch(-2), at.place(-2)
                head = at.fixed - 2 - b * HEADS
                wait(pe, wp_split, at.p - 1)
                wait(pe, y_lo_done, at.p - 1)
                if head == 0:
                    if b:
                        pe.wait_ge(out_taken, 2 * b)
                    else:
                        pe.wait_ge(k_split, BATCH)
                        pe.wait_ge(kT_done, BATCH)
                        pe.wait_ge(kT_split, BATCH)
                for j in range(TILES):
                    t = slice(j * P, (j + 1) * P)
                    last = product(ps_out[:, j, :], (yT_hi[:, t], yT_lo[:, t]), (wp_hi[s][:, :], wp_lo[s][:, :]),
                                   head == 0 and j % 2 == 0, head == HEADS - 1, True)
                    if j == 1 and at.fixed == LAST - 1:
                        last.then_inc(proj_half, 1)
                last.then_inc(proj_done, 1)

            def values(at):
                p, b = at.p, at.batch(-1)
                if at.fixed - 1 == b * HEADS:
                    pe.wait_ge(k_split, b + 1)
                    pe.wait_ge(k_last_done, b + 1)
                wait(pe, y_lo_done, p - 1)
                for i in range(TILES - 1):
                    wait(pe, pt_lo_done, p * 3 - 2 + i)
                    n = (TILES - i) * P
                    t = slice(PT_OFF[i], PT_OFF[i] + n)
                    product(ps_y[:, SEQ - n:], (k_hi[b][:, i, :], k_lo[b][:, i, :]),
                            (pT_hi[:, t], pT_lo[:, t]), i == 0, False)
                wait(pe, pt_last_done, p)
                pe.matmul(ps_y[:, SEQ - P:], k_last[b][:, :], pT_last[:, :], start=False, stop=True).then_inc(y_ready, 1)

            def turn_scores(b, dst):
                pe.wait_ge(score_done[b], 1)
                for j in range(TILES):
                    last = pe.transpose(dst[:, j * P:(j + 1) * P], score[:, b, j:j + 1].to_broadcast([P, P]), ident[:, :])
                last.then_inc(score_turned[b], 1)

            def rank_cols(b, dst):
                pe.wait_ge(compared[b], 3 * TILES - 1)
                for j in range(TILES):
                    for i in range(TILES):
                        pe.matmul(dst[:, j:j + 1], beats[:, i, j * P:(j + 1) * P], ones_bf[:, 0:1],
                                  start=(i == 0), stop=False)
                    last = pe.matmul(dst[:, j:j + 1], ties[:, j, :], ones_bf[:, 0:1], start=False, stop=True)
                last.then_inc(rank_ready[b], 1)

            def rank_rows(b, dst):
                pe.wait_ge(rank_done[b], 1)
                for j in range(TILES):
                    last = pe.transpose(dst[:, j * P:(j + 1) * P], rank[:, j:j + 1].to_broadcast([P, P]), ident[:, :])
                last.then_inc(rank_row_ready[b], 1)

            def gather(b, tiles=range(TILES)):
                pe.wait_ge(x1_split[b], 2)
                pe.wait_ge(negmax_done, 4 * UNITS)
                if b:
                    pe.wait_ge(xs_split[0], CH)
                    pe.wait_ge(gelu_done[0], FCH)
                for j in tiles:
                    pe.wait_ge(sel_done[b], j + 1)
                    for c in range(CH):
                        t, cs = b * TILES + j, slice(c * P, (c + 1) * P)
                        pe.matmul(chosen_bank(c), x1_hi[:, t, cs], sel[:, t, :], start=(j == 0), stop=False,
                                  skip_group_check=True)
                        last = pe.matmul(chosen_bank(c), x1_lo[:, t, cs], sel[:, t, :], start=False,
                                         stop=(j == TILES - 1), skip_group_check=True)
                        if j == TILES - 1:
                            last.then_inc(gathered[b], 1)

            def hidden(b, fs):
                for f in fs:
                    if f == 0:
                        pe.wait_ge(xs_split[b], CH)
                        pe.wait_ge(wf_split, len(WF_PERIODS))
                        if b:
                            pe.wait_ge(gelu_done[0], FCH)
                    if f == 3 and b == 0:
                        pe.wait_ge(y_lo_done, UNITS)
                    if f >= len(hidden_banks):
                        pe.wait_ge(gelu_done[b], f - len(hidden_banks) + 1)
                    for c in range(CH):
                        w = slice(c * FFN + f * P, c * FFN + (f + 1) * P)
                        last = product(hidden_bank(f), (wf_hi[:, w], wf_lo[:, w]),
                                       (xs_hi[:, b, c, :], xs_lo[:, b, c, :]), c == 0, c == CH - 1)
                    last.then_inc(hid_ready[b], 1)

            def start_net():
                pe.wait_ge(out_taken, 2 * BATCH)
                pe.wait_ge(consts, CONSTS)
                pe.wait_ge(b2_split, 1)
                for r in range(RCH):
                    for part in (b2_hi, b2_lo):
                        pe.matmul(ps_out[:, 2 * r:2 * r + 2, :], ones_row[:, :],
                                  part[:, :].unsqueeze(1).broadcast_to([1, BATCH, DIM]), start=part is b2_hi,
                                  stop=False, skip_group_check=True)

            def net_out(b, r, fs=range(FCH)):
                for f in fs:
                    if r == 0:
                        pe.wait_ge(hid_split[b], f + 1)
                    w = slice(W2_AT + f * DIM, W2_AT + (f + 1) * DIM)
                    t = slice(r * P, (r + 1) * P)
                    last = product(net_bank(b, r), (hid_hi[:, b, f, t], hid_lo[:, b, f, t]),
                                   (wf_hi[:, w], wf_lo[:, w]), False, f == FCH - 1, True)
                    if f == FCH - 1:
                        last.then_inc(net_ready[b], 1)

            def scatter(b):
                pe.wait_ge(selT_done[b], RCH)
                if b == 0:
                    pe.wait_ge(rank_done[1], 1)
                    pe.wait_ge(rank_row_done[1], 1)
                else:
                    pe.wait_ge(sum_done[0], TILES)
                    pe.wait_ge(gelu_done[1], FCH)
                for q in range(RCH):
                    pe.wait_ge(net_split[b], q + 1)
                    for j in range(TILES):
                        one = selT[:, b, q, j * P:(j + 1) * P]
                        dst, first = scatter_bank(b, j), q == 0 and (b > 0 or j % 2 == 0)
                        pe.matmul(dst, one, net_hi[:, b, q, :], start=first, stop=False, skip_group_check=True)
                        last = pe.matmul(dst, one, net_lo[:, b, q, :], start=False, stop=(q == RCH - 1),
                                         skip_group_check=True)
                        if q == RCH - 1 and (b or j % 2):
                            last.then_inc(scattered[b], 1)

            def period(at):
                if at.live(0):
                    scores(at, (3, 2))
                if at.fixed == 1:
                    turn_k(1)
                if at.fixed == UNITS:
                    gather(0, range(0, 2))
                if at.live(-1):
                    turn(at, 0)
                    turn(at, 1)
                if at.live(0):
                    scores(at, (1, 0))
                if at.live(1) and at.fixed >= 0:
                    queries(at)
                if at.live(1):
                    if at.live(-1):
                        turn(at, 2)
                    if at.fixed == 0:
                        project_k(1)
                    if at.live(-2):
                        project(at)
                else:
                    if at.fixed == UNITS:
                        gather(0, range(2, TILES))
                    if at.fixed == UNITS + 1:
                        hidden(0, range(0, 2))
                    if at.live(-2):
                        project(at)
                    if at.live(-1):
                        turn(at, 2)
                if at.live(-1):
                    values(at)
                if at.fixed in (AT_TURN, AT_SELECT, AT_RANK):
                    pe.wait_ge(pt_lo_done, at.p * 3 - 1)
                if at.fixed == AT_TURN:
                    turn_scores(0, ps_t1)
                if at.fixed == AT_RANK:
                    rank_cols(0, ps_t1)
                if at.fixed == AT_SELECT:
                    rank_rows(0, ps_t1)

            periods(pe, period)

            hidden(0, range(2, 6))
            start_net()
            hidden(0, range(6, FCH))
            net_out(0, 0, range(0, 4))
            turn_scores(1, ps_t0)
            net_out(0, 0, range(4, FCH))
            net_out(0, 1)
            pe.wait_ge(score_row_done[1], 1)
            rank_cols(1, ps_t0)
            rank_rows(1, ps_t1)
            gather(1)
            scatter(0)
            hidden(1, range(FCH))
            for r in range(RCH):
                net_out(1, r)
            scatter(1)

        @block.scalar
        def _(act):
            def split_queries(k, place, head):
                wait(act, q_ready, k + 1)
                wait(act, scores_ready, k * 3 - 3)
                bias = bias_cols[:, bass.ds(head, 1)]
                act.activation(qT_first[place][:, :], ps_q[:, 0:P], ACT.Identity, bias=bias,
                               scale=1.0).then_inc(q_first_done, 1)
                act.activation(qT_hi[place][:, P:], ps_q[:, P:], ACT.Identity, bias=bias,
                               scale=1.0).then_inc(q_hi_done, 1)

            def x_high(b):
                for c in range(CH):
                    act.wait_ge(x_turned, CH * b + c + 1)
                    act.copy(xT_hi[b][:, c, :], (ps_t0, ps_t1)[c][:, :]).then_inc(x_hi_done, 1)

            def kT_high(b):
                act.wait_ge(*((kT_done, b + 1) if b else (kT_ready, 1)))
                act.activation(kT_hi[b][:, :], ps_kT, ACT.Identity, bias=bias_cols[:, B_LAT:B_LAT + 1],
                               scale=1.0).then_inc(kT_hi_done, 1)

            def k_high(b):
                act.wait_ge(k_turned, b + 1)
                act.copy(k_last[b][:, :], ps_k[:, SEQ - P:]).then_inc(k_last_done, 1)
                act.copy(k_hi[b][:, :, :], ps_k[:, 0:SEQ - P].rearrange("p (j l) -> p j l", l=LAT)).then_inc(k_hi_done, 1)

            x_high(0)
            act.wait_ge(bias_done, 1)
            kT_high(0)
            split_queries(0, 0, 0)
            x_high(1)
            k_high(0)

            def exps(at, js):
                s = at.place(0)
                for j in js:
                    wait(act, negmax_done, at.p * 4 + 4 - j)
                    act.activation(p_tile(s, j), p_tile(s, j), ACT.Exp, bias=negmax[:, s, j:j + 1],
                                   scale=-1.0, accum_out=sums[:, s, j:j + 1]).then_inc(exp_done, 1)

            def turned(at, n):
                wait(act, pt_ready, at.p * 3 - 2 + n)
                if n == 2:
                    act.copy(pT_last[:, :], ps_t0[:, 0:P]).then_inc(pt_last_done, 1)
                act.copy(pT_hi[:, turns[n][3]], turns[n][2]).then_inc(pt_hi_done, 1)

            def period(at):
                p = at.p
                if at.live(-2):
                    wait(act, y_ready, p - 1)
                    wait(act, proj_done, p - 2)
                    act.copy(yT_hi[:, :], ps_y[:, :]).then_inc(y_hi_done, 1)
                if at.fixed - 1 == AT_TURN:
                    row_of_scores(0, ps_t1)
                if at.fixed - 1 == AT_RANK:
                    col_of_ranks(0, ps_t1)
                if at.fixed - 1 == AT_SELECT:
                    row_of_ranks(0, ps_t1)
                if at.fixed == 1:
                    k_high(1)
                if at.live(-1):
                    wait(act, y_ready, p - 1)
                    turned(at, 0)
                    turned(at, 1)
                if at.fixed == UNITS:
                    act.wait_ge(consts, CONSTS)
                    act.activation(gelu_first[:, :], zero[:, 0:1], ACT.Gelu_apprx_tanh)
                    chosen(0)
                if at.live(0):
                    exps(at, (3, 2))
                if at.live(1) and at.fixed >= 0:
                    split_queries(p + 1, at.place(1), at.head(1))
                if at.live(-1):
                    turned(at, 2)
                if at.live(0):
                    exps(at, (1, 0))
                    wait(act, rinv_done, p + 1)
                    act.mul(p_tile(at.place(0), 3), p_tile(at.place(0), 3),
                            rinv[:, at.place(0), 3:4]).then_inc(norm_act, 1)
                if at.fixed == 0:
                    kT_high(1)
                if at.fixed in (AT_COMPARE_2, AT_RANK):
                    x1_high(0, at.fixed - AT_COMPARE_2)

            def x1_high(b, half):
                t = slice(b * TILES + 2 * half, b * TILES + 2 * half + 2)
                act.wait_ge(ln_done[b], 2 * half + 2)
                act.copy(x1_hi[:, t, :], x1[:, t, :]).then_inc(x1_hi_done[b], 1)

            def row_of_scores(b, src):
                act.wait_ge(score_turned[b], 1)
                if b:
                    act.wait_ge(compared[0], 3 * TILES - 1)
                act.copy(score_row[:, :], src[:, :]).then_inc(score_row_done[b], 1)
                act.activation(half_tanh[:, b, :], score[:, b, :], ACT.Tanh, bias=0.0, scale=0.5).then_inc(tanh_done[b], 1)

            def row_of_ranks(b, src):
                act.wait_ge(rank_row_ready[b], 1)
                if b:
                    act.wait_ge(selT_done[0], RCH)
                act.copy(rank_row[:, :], src[:, :]).then_inc(rank_row_done[b], 1)

            def col_of_ranks(b, src):
                act.wait_ge(rank_ready[b], 1)
                if b:
                    act.wait_ge(sel_done[0], TILES)
                    act.wait_ge(rank_row_ready[0], 1)
                act.copy(rank[:, :], src[:, 0:TILES]).then_inc(rank_done[b], 1)

            def gelu(b, f):
                act.wait_ge(hid_ready[b], f + 1)
                if b:
                    act.wait_ge(hid_split[0], f + 1)
                act.activation(hid[:, f, :], hidden_bank(f), ACT.Gelu_apprx_tanh,
                               bias=bias_cols[:, B_ONE + f:B_ONE + f + 1], scale=1.0).then_inc(gelu_done[b], 1)

            def hidden_high(b, f):
                act.wait_ge(gelu_done[b], f + 1)
                act.copy(hid_hi[:, b, f, :], hid[:, f, :]).then_inc(hid_hi_done[b], 1)

            def hidden_layer(b):
                for f in range(FCH):
                    gelu(b, f)
                    if f and not (b == 0 and f == 2):
                        hidden_high(b, f - 1)
                    if b == 0 and f == 1:
                        hidden_high(b, f)
                hidden_high(b, FCH - 1)

            def chosen(b):
                for c in range(CH):
                    act.wait_ge(gathered[b], c + 1)
                    act.copy(xs_hi[:, b, c, :], chosen_bank(c)).then_inc(xs_hi_done[b], 1)

            def net_high(b, r):
                act.wait_ge(net_ready[b], r + 1)
                act.copy(net_hi[:, b, r, :], net_bank(b, r)).then_inc(net_hi_done[b], 1)

            periods(act, period)

            hidden_layer(0)
            row_of_scores(1, ps_t0)
            for half in range(2):
                x1_high(1, half)
            net_high(0, 0)
            col_of_ranks(1, ps_t0)
            row_of_ranks(1, ps_t1)
            net_high(0, 1)
            chosen(1)
            hidden_layer(1)
            for r in range(RCH):
                net_high(1, r)
            for j in range(TILES):
                act.wait_ge(minus_mean_done, j // 2 + 1)
                act.activation(squared[:, j, :], x1[:, TILES + j, :], ACT.Square, bias=minus_mean[:, j:j + 1],
                               scale=1.0, accum_out=squares[:, j:j + 1]).then_inc(squares_done, 1)

        @block.vector
        def _(dve):
            def queries_low(k, place, head):
                wait(dve, q_hi_done, k + 1)
                dve.scalar_tensor_tensor(qT_lo[place][:, P:], ps_q[:, P:], bias_cols[:, bass.ds(head, 1)],
                                         qT_hi[place][:, P:].bitcast(F32), ALU.add, ALU.subtract).then_inc(q_lo_done, 1)

            dve.memset(still[:, :], 0.0).then_inc(still_filled, 1)

            def x_low(b, c):
                dve.wait_ge(x_hi_done, CH * b + c + 1)
                dve.tensor_tensor(xT_lo[b][:, c, :], (ps_t0, ps_t1)[c][:, :],
                                  xT_hi[b][:, c, :].bitcast(F32), ALU.subtract).then_inc(x_split, 1)

            def kT_bias(b):
                dve.wait_ge(kT_ready, b + 1)
                dve.tensor_scalar(kT[b][:, :], ps_kT, bias_cols[:, B_LAT:B_LAT + 1], None,
                                  ALU.add).then_inc(kT_done, 1)

            def kT_low(b):
                dve.wait_ge(kT_hi_done, b + 1)
                dve.scalar_tensor_tensor(kT_lo[b][:, :], ps_kT, bias_cols[:, B_LAT:B_LAT + 1],
                                         kT_hi[b][:, :].bitcast(F32), ALU.add, ALU.subtract).then_inc(kT_split, 1)

            def k_low(b):
                dve.wait_ge(k_hi_done, b + 1)
                dve.tensor_tensor(k_lo[b][:, :, :], ps_k[:, 0:SEQ - P].rearrange("p (j l) -> p j l", l=LAT),
                                  k_hi[b][:, :, :].bitcast(F32), ALU.subtract).then_inc(k_split, 1)

            dve.wait_ge(wlat_in, 16)
            dve.tensor_copy(wlat_hi[:], wlat_raw[:]).then_inc(wlat_hi_done, 1)
            dve.wait_ge(wlat_hi_done, 1)
            dve.tensor_tensor(wlat_lo[:], wlat_raw[:], wlat_hi[:].bitcast(F32), ALU.subtract).then_inc(wlat_split, 1)
            for c in range(CH):
                x_low(0, c)
            dve.wait_ge(bias_turned, 1)
            dve.tensor_copy(bias_cols[:, :], ps_s2[:, 0:BIASES]).then_inc(bias_done, 1)
            dve.wait_ge(bias_done, 1)
            kT_low(0)
            kT_bias(0)
            queries_low(0, 0, 0)
            x_low(1, 0)
            dve.wait_ge(mask_done, 1)

            def maxima(at, js):
                s = at.place(0)
                for j in js:
                    dve.tensor_tensor_reduce(p_tile(s, j), score_bank[j], mask_row[:, (TILES - 1 - j) * P:],
                                             -SCALE, -MASKED, ALU.add, ALU.min,
                                             accum_out=negmax[:, s, j:j + 1]).then_inc(negmax_done, 1)

            def turned(at, n):
                wait(dve, pt_hi_done, at.p * 3 - 2 + n)
                _, _, src, dst = turns[n]
                dve.tensor_tensor(pT_lo[:, dst], src, pT_hi[:, dst].bitcast(F32), ALU.subtract).then_inc(pt_lo_done, 1)

            def period(at):
                p = at.p
                if at.live(0):
                    wait(dve, scores_ready, p * 3 + 1)
                if at.live(-2):
                    wait(dve, y_hi_done, p - 1)
                    dve.tensor_tensor(yT_lo[:, :], ps_y[:, :], yT_hi[:, :].bitcast(F32),
                                      ALU.subtract).then_inc(y_lo_done, 1)
                if at.live(0):
                    maxima(at, (3,))
                early_piece(at)
                if at.live(0):
                    wait(dve, scores_ready, p * 3 + 2)
                if at.live(-1):
                    turned(at, 0)
                if at.live(0):
                    maxima(at, (2,))
                    wait(dve, scores_ready, p * 3 + 3)
                if at.live(-1):
                    turned(at, 1)
                if at.fixed == UNITS:
                    chosen_low(0)
                if at.live(0):
                    maxima(at, (1, 0))
                if at.fixed == 0:
                    x_low(1, 1)
                    k_low(0)
                if at.live(1) and at.fixed >= 0:
                    queries_low(p + 1, at.place(1), at.head(1))
                if at.fixed == 0:
                    kT_bias(1)
                if at.live(-1):
                    turned(at, 2)
                s = at.place(0)
                if at.live(0):
                    wait(dve, exp_done, p * 4 + 4)
                    dve.reciprocal(rinv[:, s, :], sums[:, s, :]).then_inc(rinv_done, 1)
                late_piece(at)
                if at.live(0):
                    wait(dve, rinv_done, p + 1)
                    for j in (2, 1, 0):
                        dve.tensor_scalar(p_tile(s, j), p_tile(s, j), rinv[:, s, j:j + 1], None,
                                          ALU.mult).then_inc(norm_dve, 1)

            def early_piece(at):
                if at.fixed == 1:
                    k_low(1)
                if at.fixed == AT_STATS:
                    take_out(0, 1)
                if at.fixed == AT_VARIANCE:
                    layernorm_stats(0, 0, 1)
                if at.fixed == AT_APPLY:
                    layernorm_apply(0, 0, 0)
                if at.fixed == AT_SCORE:
                    router_dots(0, 0)
                if at.fixed == AT_TURN:
                    router_scores(0)
                if at.fixed == AT_COMPARE:
                    compare(0, (0,))
                if at.fixed == AT_COMPARE_2:
                    compare(0, (2,))
                if at.fixed == AT_SELECT:
                    select(0, range(0, 2))
                if at.fixed == AT_SELECT_T:
                    select_turned(0, 0)

            def late_piece(at):
                if at.fixed == 1:
                    kT_low(1)
                if at.fixed == AT_OUT:
                    take_out(0, 0)
                if at.fixed == AT_STATS:
                    layernorm_stats(0, 0, 0)
                if at.fixed == AT_VARIANCE:
                    for half in range(2):
                        variance(0, 0, half)
                if at.fixed == AT_APPLY:
                    layernorm_apply(0, 0, 1)
                if at.fixed == AT_SCORE:
                    router_dots(0, 1)
                if at.fixed == AT_COMPARE:
                    compare(0, (1,))
                if at.fixed == AT_COMPARE_2:
                    compare(0, (3,))
                if at.fixed == AT_SELECT:
                    select(0, range(2, TILES))
                if at.fixed == AT_SELECT_T:
                    select_turned(0, 1)
                    weights(0)

            def take_out(b, half):
                dve.wait_ge(*((proj_half, 1) if b and half == 0 else (proj_done, (b + 1) * HEADS)))
                dve.wait_ge(x1_started, b + 1)
                t = slice(b * TILES + 2 * half, b * TILES + 2 * half + 2)
                dve.tensor_tensor(x1[:, t, :], ps_out[:, 2 * half:2 * half + 2, :], x1[:, t, :],
                                  ALU.add).then_inc(out_taken, 1)

            def layernorm_stats(b, which, half):
                k = which * BATCH + b
                tiles = range(2 * half, 2 * half + 2)
                if which == 0:
                    dve.wait_ge(out_taken, 2 * b + half + 1)
                for j in tiles:
                    if which:
                        dve.wait_ge(sum_done[b], j + 1)
                    dve.bn_stats(st[:, k, j, :], x1[:, b * TILES + j, :]).then_inc(stats_done[b], 1)

            def variance(b, which, half):
                k = which * BATCH + b
                for j in range(2 * half, 2 * half + 2):
                    dve.wait_ge(stats_done[b], which * TILES + j + 1)
                    dve.bn_aggr(mv[:, k, j, :], st[:, k, j, :]).then_inc(aggr_done[b], 1)
                dve.wait_ge(aggr_done[b], which * TILES + 2 * half + 2)
                t = slice(2 * half, 2 * half + 2)
                dve.tensor_scalar(ve[:, k, t], mv[:, k, t, 1], EPS, None, ALU.add).then_inc(var_done[b], 1)

            def layernorm_apply(b, which, half):
                k = which * BATCH + b
                dve.wait_ge(rstd_done[b], 2 * which + half + 1)
                for j in range(2 * half, 2 * half + 2):
                    r = x1[:, b * TILES + j, :]
                    dve.tensor_scalar(r, r, mv[:, k, j, 0:1], rstd[:, k, j:j + 1],
                                      ALU.subtract, ALU.mult).then_inc(ln_done[b], 1)

            def router_dots(b, half):
                if b == 0:
                    dve.wait_ge(consts, CONSTS)
                for j in range(2 * half, 2 * half + 2):
                    dve.wait_ge(ln_done[b], j + 1)
                    dve.scalar_tensor_tensor(sel[:, b * TILES + j, :], x1[:, b * TILES + j, :], 1.0,
                                             rw_all[:, :], ALU.mult, ALU.mult,
                                             accum_out=dots[:, b, j:j + 1]).then_inc(dots_done[b], 1)

            def router_scores(b):
                dve.wait_ge(dots_done[b], TILES)
                dve.tensor_scalar(score[:, b, :], dots[:, b, :], rb_all[:, 0:1], None, ALU.add).then_inc(score_done[b], 1)

            def compare(b, tiles):
                dve.wait_ge(score_row_done[b], 1)
                if b:
                    dve.wait_ge(rank_ready[0], 1)
                for t in tiles:
                    mine, own = score[:, b, t:t + 1], (t + 1) * P
                    dve.tensor_scalar(beats[:, t, 0:own], score_row[:, 0:own], mine, None,
                                      ALU.is_lt).then_inc(compared[b], 1)
                    if own < SEQ:
                        dve.tensor_scalar(beats[:, t, own:], score_row[:, own:], mine, None,
                                          ALU.is_le).then_inc(compared[b], 1)
                    dve.scalar_tensor_tensor(ties[:, t, :], score_row[:, t * P:own], mine, earlier[:, :],
                                             ALU.is_equal, ALU.mult).then_inc(compared[b], 1)

            def select(b, tiles):
                dve.wait_ge(rank_done[b], 1)
                for j in tiles:
                    dve.tensor_scalar(sel[:, b * TILES + j, :], iota_row[:, :], rank[:, j:j + 1], None,
                                      ALU.is_equal).then_inc(sel_done[b], 1)

            def select_turned(b, q):
                dve.wait_ge(rank_row_done[b], 1)
                dve.tensor_scalar(selT[:, b, q, :], rank_row[:, :], iota_col[:, q:q + 1], None,
                                  ALU.is_equal).then_inc(selT_done[b], 1)

            def weights(b):
                dve.wait_ge(tanh_done[b], 1)
                dve.tensor_scalar(weight[:, b, :], half_tanh[:, b, :], 0.5, 0.5, ALU.mult, ALU.add).then_inc(weight_done[b], 1)

            def chosen_low(b):
                for c in range(CH):
                    dve.wait_ge(xs_hi_done[b], c + 1)
                    dve.tensor_tensor(xs_lo[:, b, c, :], chosen_bank(c),
                                      xs_hi[:, b, c, :].bitcast(F32), ALU.subtract).then_inc(xs_split[b], 1)

            def net_low(b, r):
                dve.wait_ge(net_hi_done[b], r + 1)
                dve.tensor_tensor(net_lo[:, b, r, :], net_bank(b, r), net_hi[:, b, r, :].bitcast(F32),
                                  ALU.subtract).then_inc(net_split[b], 1)

            def add_up(b, j):
                if j == 0:
                    dve.wait_ge(weight_done[b], 1)
                    dve.wait_ge(x1_doubled[b], 1)
                r = x1[:, b * TILES + j, :]
                dve.wait_ge(scattered[b], j + 1 if b else j // 2 + 1)
                dve.scalar_tensor_tensor(r, scatter_bank(b, j),
                                         weight[:, b, j:j + 1], r, ALU.mult, ALU.add,
                                         accum_out=z_sum[:, j:j + 1]).then_inc(sum_done[b], 1)

            periods(dve, period)

            for half in range(2):
                take_out(1, half)
                layernorm_stats(1, 0, half)
                variance(1, 0, half)
            for half in range(2):
                layernorm_apply(1, 0, half)
                router_dots(1, half)
            router_scores(1)
            compare(1, range(TILES))
            net_low(0, 0)
            select(1, range(TILES))
            net_low(0, 1)
            chosen_low(1)
            for q in range(RCH):
                select_turned(1, q)
            weights(1)
            for f in range(FCH):
                dve.wait_ge(hid_hi_done[1], f + 1)
                dve.tensor_tensor(hid_lo[:, 1, f, :], hid[:, f, :], hid_hi[:, 1, f, :].bitcast(F32),
                                  ALU.subtract).then_inc(hid_split[1], 1)
                if f < TILES:
                    add_up(0, f)
            for half in range(2):
                layernorm_stats(0, 1, half)
                variance(0, 1, half)
            net_low(1, 0)
            for half in range(2):
                layernorm_apply(0, 1, half)
            net_low(1, 1)
            for half in range(2):
                for j in range(2 * half, 2 * half + 2):
                    add_up(1, j)
                t = slice(2 * half, 2 * half + 2)
                dve.wait_ge(sum_done[1], 2 * half + 2)
                dve.tensor_scalar(minus_mean[:, t], z_sum[:, t], -1.0 / DIM, None,
                                  ALU.mult).then_inc(minus_mean_done, 1)
            for half in range(2):
                t = slice(2 * half, 2 * half + 2)
                dve.wait_ge(squares_done, 2 * half + 2)
                dve.tensor_scalar(ve[:, 2 * BATCH - 1, t], squares[:, t], 1.0 / DIM, EPS,
                                  ALU.mult, ALU.add).then_inc(var_done[1], 1)
            for half in range(2):
                dve.wait_ge(rstd_done[1], 2 + half + 1)
                for j in range(2 * half, 2 * half + 2):
                    z = x1[:, TILES + j, :]
                    dve.tensor_scalar(z, z, minus_mean[:, j:j + 1], rstd[:, 2 * BATCH - 1, j:j + 1],
                                      ALU.add, ALU.mult).then_inc(ln_done[1], 1)

        @block.gpsimd
        def _(pool):
            def split(hi, lo, src, hi_done, split_done, number):
                nothing = zero[0:src.shape[0], 0:src.free_size()]
                if len(src.shape) == 3:
                    nothing = nothing.rearrange("p (a c) -> p a c", a=src.shape[1])
                pool.tensor_tensor(hi, src, nothing, ALU.add).then_inc(hi_done, 1)
                wait(pool, hi_done, number + 1)
                pool.tensor_tensor(lo, src, hi.bitcast(F32), ALU.subtract).then_inc(split_done, 1)

            def split_wd(unit, place, use):
                wait(pool, wd_in[place], (use + 1) * 16)
                wait(pool, q_ready, unit - 1)
                split(wd_hi[place][:], wd_lo[place][:], wd_raw[place][:], wd_hi_done, wd_split, unit)

            pool.memset(ident[:, :], 0.0).then_inc(filled, 1)
            pool.memset(zero[:, :], 0.0).then_inc(filled, 1)
            pool.wait_ge(filled, 2)
            pool.affine_select(out=ident[:, :], in_=ident[:, :], compare_op=ALU.not_equal, fill=1.0, base=0,
                               pattern=[[-1, P]], channel_multiplier=1).then_inc(ident_done, 1)
            split_wd(0, 0, 0)
            pool.memset(mask_row[:, :], 0.0).then_inc(filled, 1)
            pool.memset(earlier[:, :], 1.0).then_inc(filled, 1)
            pool.wait_ge(filled, 4)
            last = mask_row[:, SEQ - P:]
            pool.affine_select(out=last, in_=last, compare_op=ALU.is_ge, fill=MASKED, base=0,
                               pattern=[[-1, P]], channel_multiplier=1).then_inc(mask_done, 1)
            pool.affine_select(out=earlier[:, :], in_=earlier[:, :], compare_op=ALU.is_gt, fill=0.0,
                               base=0, pattern=[[1, P]], channel_multiplier=-1).then_inc(consts, 1)

            def period(at):
                if at.live(2):
                    split_wd(at.p + 2, at.place(2), at.use(2))
                if at.live(-1):
                    s = at.place(-1)
                    wait(pool, wp_in[s], (at.use(-1) + 1) * 16)
                    wait(pool, proj_done, at.p - 2)
                    split(wp_hi[s][:], wp_lo[s][:], wp_raw[s][:], wp_hi_done, wp_split, at.p - 1)
                if at.fixed in (0, 1):
                    start_x1(at.fixed)
                if at.fixed == 1:
                    pool.memset(ones_bf[:, :], 1.0).then_inc(consts, 1)
                    pool.iota(iota_row[:, :], pattern=[[1, KEEP]], base=0, channel_multiplier=0,
                              allow_small_or_imprecise_dtypes=True).then_inc(consts, 1)
                    pool.iota(iota_col[:, :], pattern=[[P, RCH]], base=0, channel_multiplier=1,
                              allow_small_or_imprecise_dtypes=True).then_inc(consts, 1)
                    pool.memset(minus_half[:, :], -0.5).then_inc(consts, 1)
                    pool.memset(ones_row[:, :].bitcast(F32), 1.0).then_inc(consts, 1)
                    pool.wait_ge(rows_in, 64)
                    split(b2_hi[:, :], b2_lo[:, :], b2_all[0:1, :], b2_hi_done, b2_split, 0)
                if at.fixed in WF_PERIODS:
                    n = WF_PERIODS.index(at.fixed)
                    if n == 0:
                        pool.wait_ge(w1_in, 16)
                        pool.wait_ge(w2_in, 16)
                    part = slice(n * WF_PART, (n + 1) * WF_PART)
                    split(wf_hi[:, part], wf_lo[:, part], wf_raw[:, part], wf_hi_done, wf_split, n)
                if at.fixed == AT_VARIANCE:
                    for half in range(2):
                        inverse_deviation(0, 0, half)
                if at.fixed in (AT_COMPARE_2, AT_RANK):
                    x1_low(0, at.fixed - AT_COMPARE_2)
                if at.fixed == AT_SELECT_T:
                    double_x1(0)

            def start_x1(b):
                for half in range(2):
                    pool.wait_ge(x_in[b][half], 16)
                pool.wait_ge(rows_in, 64)
                pool.tensor_tensor(x1_of(b), x_nat[:, b * TILES:(b + 1) * TILES, :],
                                   bproj_all[:, :].unsqueeze(1).broadcast_to([P, TILES, DIM]),
                                   ALU.add).then_inc(x1_started, 1)

            def inverse_deviation(b, which, half):
                k = which * BATCH + b
                t = slice(2 * half, 2 * half + 2)
                pool.wait_ge(consts, CONSTS)
                pool.wait_ge(var_done[b], 2 * which + half + 1)
                pool.tensor_tensor(rstd[:, k, t], ve[:, k, t], minus_half[:, t], ALU.pow).then_inc(rstd_done[b], 1)

            def x1_low(b, half):
                t = slice(b * TILES + 2 * half, b * TILES + 2 * half + 2)
                pool.wait_ge(x1_hi_done[b], half + 1)
                pool.tensor_tensor(x1_lo[:, t, :], x1[:, t, :], x1_hi[:, t, :].bitcast(F32),
                                   ALU.subtract).then_inc(x1_split[b], 1)

            def double_x1(b):
                pool.wait_ge(x1_split[b], 2)
                pool.wait_ge(dots_done[b], TILES)
                pool.tensor_tensor(x1_of(b), x1_of(b), x1_of(b), ALU.add).then_inc(x1_doubled[b], 1)

            def hidden_low(f):
                pool.wait_ge(hid_hi_done[0], f + 1)
                pool.tensor_tensor(hid_lo[:, 0, f, :], hid[:, f, :], hid_hi[:, 0, f, :].bitcast(F32),
                                   ALU.subtract).then_inc(hid_split[0], 1)

            periods(pool, period)
            for f in range(FCH):
                if f in (2, 3):
                    inverse_deviation(1, 0, f - 2)
                hidden_low(f)
            for half in range(2):
                x1_low(1, half)
            double_x1(1)
            for b in range(BATCH):
                for half in range(2):
                    inverse_deviation(b, 1, half)
    return nc


_INS = ["L0_attn_x", "L0_attn_W_lat", "L0_attn_b_lat", "L0_attn_W_d", "L0_attn_b_d", "L0_attn_W_proj",
        "L0_attn_b_proj", "L0_ffn_router_weight", "L0_ffn_router_bias", "L0_ffn_w1", "L0_ffn_b1",
        "L0_ffn_w2", "L0_ffn_b2"]


def kernel(**inputs):
    import numpy as np
    from concourse import bacc
    from concourse.bass_utils import run_bass_kernel_spmd

    nc = bacc.Bacc("TRN2", target_bir_lowering=False, num_devices=1)
    arrays, args = {}, []
    for name in _INS:
        a = np.ascontiguousarray(inputs[name])
        arrays[f"in_{name}"] = a
        args.append(nc.dram_tensor(f"in_{name}", a.shape, mybir.dt.from_np(a.dtype), kind="ExternalInput").ap())
    out = nc.dram_tensor("out", (BATCH, SEQ, DIM), F32, kind="ExternalOutput").ap()
    mk_layer_kernel(nc, *args, out)
    r = run_bass_kernel_spmd(nc, [arrays], core_ids=[0])
    return r.results[0]["out"]
```
